# Optimizing a Trainium2 kernel written in Bass

```python
import numpy as np
import jax
import jax.numpy as jnp

def _softmax(x, axis=-1):
    return jax.nn.softmax(x, axis=axis)

def _gelu(x):
    return jax.nn.gelu(x, approximate=True)

def _silu(x):
    return jax.nn.silu(x)

def _sigmoid(x):
    return jax.nn.sigmoid(x)

def _layernorm(x, axis=-1, eps=1e-05):
    m = jnp.mean(x, axis=axis, keepdims=True)
    v = jnp.var(x, axis=axis, keepdims=True)
    return (x - m) / jnp.sqrt(v + eps)

def _scatter_add(tgt, idx, src, axis=0):
    return tgt.at[idx].add(src)

def _segment_sum(src, seg, n):
    return jax.ops.segment_sum(src, seg, n)
kernel_name = 'mk_adj_resnorm_d4_adj_r2_097ff6'

def setup_inputs(seed: int=0):
    np.random.seed(seed)
    _w = jnp.asarray

    def _rec_inputs():
        import jax
        import jax.numpy as jnp
        _gk = jax.random.key(seed)
        x = -0.000929 + 1 * jax.random.normal(jax.random.fold_in(_gk, 1), (4096, 128), jnp.float32)
        _w = (1.0 + jnp.arange(4096, dtype=jnp.float32)) ** (-0.5)
        _w = _w / _w.mean()
        _pij = jnp.clip(0.00195312 * _w[:, None] * _w[None, :], 0.0, 1.0)
        _a = jax.random.uniform(jax.random.fold_in(_gk, 2), (4096, 4096)) < _pij
        _a = jnp.logical_or(_a, jnp.eye(4096, dtype=bool))
        _af = _a.astype(jnp.float32)
        _af = _af * jax.random.uniform(jax.random.fold_in(_gk, 3), (4096, 4096), jnp.float32, 0.05, 1)
        adj = _af
        return (x, adj)
    x, adj = _rec_inputs()

    def _L0_gnn_setup():
        import jax, jax.numpy as jnp
        import numpy as np
        N = 4096
        H = 128
        key = jax.random.key(seed)
        k_x, k_A, k_W = jax.random.split(key, 3)
        x = jax.random.normal(k_x, (N, H), dtype=jnp.float32)
        A = jax.random.uniform(k_A, (N, N), dtype=jnp.float32)
        alpha = jnp.array([0.5], dtype=jnp.float32)
        bound = 1.0 / np.sqrt(H)
        W = jax.random.uniform(k_W, (H, H), dtype=jnp.float32, minval=-bound, maxval=bound)
        b = jnp.zeros((H,), dtype=jnp.float32)
        t = jnp.zeros((1,), dtype=jnp.float32)
        return {'t': t, 'x': x, 'A': A, 'alpha': alpha, 'W': W, 'b': b}
    _L0_gnn_all = _L0_gnn_setup()
    _L0_gnn_in = {k: v for k, v in _L0_gnn_all.items() if k in ('t', 'alpha', 'W', 'b')}
    del _L0_gnn_all

    def _L1_gnn_setup():
        import jax, jax.numpy as jnp
        import numpy as np
        N = 8192
        IN_DIM = 128
        OUT_DIM = 128

        def _message(X, A, W):
            deg = jnp.sum(A, axis=1, keepdims=True)
            A_norm = A / jnp.where(deg > 0, deg, 1.0)
            return A_norm @ X @ W
        key = jax.random.key(seed)
        k1, k2, k3, k4 = jax.random.split(key, 4)
        X = jax.random.normal(k1, (N, IN_DIM), dtype=jnp.float32)
        A = jax.random.uniform(k2, (N, N), dtype=jnp.float32)
        W_in = jax.random.normal(k3, (IN_DIM, OUT_DIM), dtype=jnp.float32) / np.sqrt(IN_DIM)
        W_out = jax.random.normal(k4, (IN_DIM, OUT_DIM), dtype=jnp.float32) / np.sqrt(IN_DIM)
        return {'X': X, 'A': A, 'W_in': W_in, 'W_out': W_out}
    _L1_gnn_all = _L1_gnn_setup()
    _L1_gnn_in = {k: v for k, v in _L1_gnn_all.items() if k in ('W_in', 'W_out')}
    del _L1_gnn_all

    def _L2_gnn_setup():
        import jax, jax.numpy as jnp
        import numpy as np
        N, NFEAT, NHID, NOUT = (4096, 128, 128, 128)
        EDGE_PROB = 0.004

        def _gcn_norm_dense(adj):
            n = adj.shape[0]
            A = adj + jnp.eye(n, dtype=adj.dtype)
            deg = A.sum(axis=1)
            d = jnp.where(deg > 0, jax.lax.rsqrt(deg), 0.0)
            return d[:, None] * A * d[None, :]
        key = jax.random.key(seed)
        k_x, k_a, k_w1, k_w2 = jax.random.split(key, 4)
        x = jax.random.normal(k_x, (N, NFEAT), dtype=jnp.float32)
        a = jax.random.uniform(k_a, (N, N), dtype=jnp.float32)
        adj = jnp.where(a < EDGE_PROB, a, 0.0)
        adj = adj.at[jnp.diag_indices(N)].set(0.0)
        W1 = jax.random.normal(k_w1, (NFEAT, NHID), dtype=jnp.float32) * (1.0 / np.sqrt(NFEAT))
        b1 = jnp.zeros((NHID,), dtype=jnp.float32)
        W2 = jax.random.normal(k_w2, (NHID, NOUT), dtype=jnp.float32) * (1.0 / np.sqrt(NHID))
        b2 = jnp.zeros((NOUT,), dtype=jnp.float32)
        return {'x': x, 'adj': adj, 'W1': W1, 'b1': b1, 'W2': W2, 'b2': b2}
    _L2_gnn_all = _L2_gnn_setup()
    _L2_gnn_in = {k: v for k, v in _L2_gnn_all.items() if k in ('W1', 'b1', 'W2', 'b2')}
    del _L2_gnn_all

    def _L3_gnn_setup():
        import jax, jax.numpy as jnp
        import numpy as np
        N, F, C, H = (4096, 128, 64, 2)
        NEG_MASK = -10000000000.0
        key = jax.random.key(seed)
        ks = jax.random.split(key, 6)
        X = jax.random.normal(ks[0], (N, F), dtype=jnp.float32)
        A = (jax.random.uniform(ks[1], (N, N)) < 0.01).astype(jnp.float32)
        diag = jnp.arange(N)
        A = A.at[diag, diag].set(1.0)
        W = jax.random.normal(ks[2], (H, F, C), dtype=jnp.float32) * 0.1
        a_self = jax.random.normal(ks[3], (H, C), dtype=jnp.float32) * 0.1
        a_neigh = jax.random.normal(ks[4], (H, C), dtype=jnp.float32) * 0.1
        b = jnp.zeros((H, C), dtype=jnp.float32)
        return {'X': X, 'A': A, 'W': W, 'a_self': a_self, 'a_neigh': a_neigh, 'b': b}
    _L3_gnn_all = _L3_gnn_setup()
    _L3_gnn_in = {k: v for k, v in _L3_gnn_all.items() if k in ('W', 'a_self', 'a_neigh', 'b')}
    del _L3_gnn_all
    return {'x': x, 'adj': adj, 'L0_gnn_t': _L0_gnn_in['t'], 'L0_gnn_alpha': _L0_gnn_in['alpha'], 'L0_gnn_W': _L0_gnn_in['W'], 'L0_gnn_b': _L0_gnn_in['b'], 'L1_gnn_W_in': _L1_gnn_in['W_in'], 'L1_gnn_W_out': _L1_gnn_in['W_out'], 'L2_gnn_W1': _L2_gnn_in['W1'], 'L2_gnn_b1': _L2_gnn_in['b1'], 'L2_gnn_W2': _L2_gnn_in['W2'], 'L2_gnn_b2': _L2_gnn_in['b2'], 'L3_gnn_W': _L3_gnn_in['W'], 'L3_gnn_a_self': _L3_gnn_in['a_self'], 'L3_gnn_a_neigh': _L3_gnn_in['a_neigh'], 'L3_gnn_b': _L3_gnn_in['b']}

def reference(x, adj, L0_gnn_t, L0_gnn_alpha, L0_gnn_W, L0_gnn_b, L1_gnn_W_in, L1_gnn_W_out, L2_gnn_W1, L2_gnn_b1, L2_gnn_W2, L2_gnn_b2, L3_gnn_W, L3_gnn_a_self, L3_gnn_a_neigh, L3_gnn_b):
    import jax
    import jax.numpy as jnp

    def _L0_gnn_ref(t, x, A, alpha, W, b):
        import jax, jax.numpy as jnp
        import numpy as np
        N = 4096
        H = 128
        a = alpha[0]
        A_prime = a * A
        diag = jnp.diagonal(A_prime) + (1.0 - a)
        A_prime = A_prime.at[jnp.arange(N), jnp.arange(N)].set(diag)
        out_degree = A_prime.sum(axis=1)
        inv_deg = jnp.where(out_degree == 0.0, 0.0, 1.0 / out_degree)
        x = inv_deg[:, None] * A_prime @ x
        x = x @ W.T + b
        return jax.nn.relu(x)

    def _L1_gnn_ref(X, A, W_in, W_out):
        import jax, jax.numpy as jnp
        import numpy as np
        N = 8192
        IN_DIM = 128
        OUT_DIM = 128

        def _message(X, A, W):
            deg = jnp.sum(A, axis=1, keepdims=True)
            A_norm = A / jnp.where(deg > 0, deg, 1.0)
            return A_norm @ X @ W
        X_in = _message(X, A, W_in)
        X_out = _message(X, A.T, W_out)
        return X_in + X_out

    def _L2_gnn_ref(x, adj, W1, b1, W2, b2):
        import jax, jax.numpy as jnp
        import numpy as np
        N, NFEAT, NHID, NOUT = (4096, 128, 128, 128)
        EDGE_PROB = 0.004

        def _gcn_norm_dense(adj):
            n = adj.shape[0]
            A = adj + jnp.eye(n, dtype=adj.dtype)
            deg = A.sum(axis=1)
            d = jnp.where(deg > 0, jax.lax.rsqrt(deg), 0.0)
            return d[:, None] * A * d[None, :]
        An = _gcn_norm_dense(adj)
        h = jax.nn.relu(An @ (x @ W1) + b1)
        out = An @ (h @ W2) + b2
        return out

    def _L3_gnn_ref(X, A, W, a_self, a_neigh, b):
        import jax, jax.numpy as jnp
        import numpy as np
        N, F, C, H = (4096, 128, 64, 2)
        NEG_MASK = -10000000000.0
        feats = jnp.einsum('nf,hfc->hnc', X, W)
        s = jnp.einsum('hnc,hc->hn', feats, a_self)
        t = jnp.einsum('hnc,hc->hn', feats, a_neigh)
        scores = s[:, :, None] + t[:, None, :]
        scores = jnp.where(scores >= 0, scores, 0.2 * scores)
        scores = scores + NEG_MASK * (1.0 - A)[None]
        attn = jax.nn.softmax(scores, axis=-1)
        out = jnp.einsum('hnm,hmc->hnc', attn, feats) + b[:, None, :]
        out = jnp.transpose(out, (1, 0, 2)).reshape(N, H * C)
        return jax.nn.relu(out)
    x = _layernorm(x + _L0_gnn_ref(L0_gnn_t, x, adj, L0_gnn_alpha, L0_gnn_W, L0_gnn_b), axis=-1)
    x = _layernorm(x + _L1_gnn_ref(x, adj, L1_gnn_W_in, L1_gnn_W_out), axis=-1)
    x = _layernorm(x + _L2_gnn_ref(x, adj, L2_gnn_W1, L2_gnn_b1, L2_gnn_W2, L2_gnn_b2), axis=-1)
    x = _layernorm(x + _L3_gnn_ref(x, adj, L3_gnn_W, L3_gnn_a_self, L3_gnn_a_neigh, L3_gnn_b), axis=-1)
    return x

_drawn_inputs = setup_inputs


def setup_inputs(seed=0):
    import zlib

    import numpy as np

    out = dict(_drawn_inputs(seed))
    spreads = {'L0_gnn_b': (0.0, 0.1),
     'L2_gnn_b1': (0.0, 0.1),
     'L2_gnn_b2': (0.0, 0.1),
     'L3_gnn_b': (0.0, 0.1)}
    factors = {}
    for name, (base, spread) in spreads.items():
        noise = np.random.default_rng([zlib.crc32(name.encode()), seed]).standard_normal(out[name].shape)
        drawn = base * np.exp(spread * noise) if base else spread * noise
        out[name] = jnp.asarray(drawn.astype(out[name].dtype))
    for name, factor in factors.items():
        out[name] = (out[name] * factor).astype(out[name].dtype)
    return out
```

```python
import concourse.bass as bass
from concourse import mybir
from contextlib import ExitStack


def graph_stack(nc, x_in, adj, alpha, w0, b0, w_in, w_out, w1, b1, w2, b2, w3, a_self, a_neigh, b3, out):
    f32, f16 = mybir.dt.float32, mybir.dt.float16
    ALU = mybir.AluOpType
    ACT = mybir.ActivationFunctionType
    AX = mybir.AxisListType
    ds = bass.ds

    P = 128
    N, D = x_in.shape
    NB = N // P
    HEADS = w3.shape[0]
    C = w3.shape[2]
    EPS = 1e-5
    NEG_MASK = 1e10
    LEAK = 0.2
    LOWEST = -3.0e38

    NS = NB // 2
    NCH = 4
    MC = NB // NCH
    J = NB // 2
    SPC = J // NCH
    CW = MC * P
    W = 2 * P
    K3 = N // 512
    U3 = 2 * K3
    J_E1 = 3 if J >= 16 else 1
    J_STAT = J_E1 + 1
    J_NORM = J_STAT + 2 if J >= 16 else J_STAT
    J_P3 = J_NORM + 1 if J >= 16 else J_NORM
    J_X0 = J // 2
    if J >= 16:
        SPLIT = {5: [(0, 0)], 6: [(0, 1)], 7: [(1, 0)], 8: [(1, 1)], 10: [(2, 0)], 11: [(2, 1)],
                 13: [(3, 0)], 15: [(3, 1)]}
    else:
        SPLIT = {c * SPC + SPC - 1: [(c, 0), (c, 1)] for c in range(NCH)}

    def units_at(j):
        def upto(k):
            return -(-U3 * max(0, k - J_P3 + 1) // (J - J_P3))
        return range(upto(j - 1), upto(j))

    NQ = NB // 4
    Q = 4
    QW = Q * P

    KV = 4
    VW = N // KV
    G4 = NB // 4
    PIECES = HEADS * KV
    BIAS_BY_DVE = [1, 3]
    if G4 == 8:
        BY_ACT = [0, 1, 3, 4]
        ACT_PLAN = "L0 L1 L2 L3 T0 L4 T1 L5 X0 T3 L6 L7 T4 X1"
        DVE_PLAN = "S0 S1 V0 S2 S3 V1 S4 V2 S5 V3 S6 V4 S7 M0 V5 V6 V7"
    else:
        BY_ACT = [0]
        ACT_PLAN = "L0 L1 L2 L3 T0 L4 L5 X0 L6 L7 X1"
        DVE_PLAN = "S0 S1 V0 S2 S3 V1 S4 S5 S6 S7 M0 " + " ".join(f"V{g}" for g in range(2, G4))

    at_dram = nc.dram_tensor("at_parts", [NS, NCH, P, MC * 2 * W], f16, kind="Internal").ap()

    ctx = ExitStack()
    with ctx:
        KB = 256
        block_kb = NB * P * 4 // 1024
        words = 12 * block_kb * KB
        arena = ctx.enter_context(nc.sbuf_tensor("arena", [P, words], f32))

        def view(at, size, dt=f32):
            v = arena[:, int(at * NB * P):int((at + size) * NB * P)]
            return v if dt is f32 else v.bitcast(dt)

        def sb(name, shape, dt=f32):
            return ctx.enter_context(nc.sbuf_tensor(name, shape, dt))

        x_nat = view(0, 1).rearrange("p (b d) -> p b d", d=D)
        at_x1 = view(1, 1)
        y_nat = view(1, 1).rearrange("p (b d) -> p b d", d=D)
        op_even = view(2, 1, f16).rearrange("p (b l d) -> p b l d", l=2, d=D)
        op_odd = view(3, 1, f16).rearrange("p (b l d) -> p b l d", l=2, d=D)
        a_in = view(4, 2).rearrange("p (c r m) -> p c r m", c=NCH, r=2)
        split = [view(8, 2, f16).rearrange("p (r l m) -> p r l m", r=2, l=2),
                 view(6, 2, f16).rearrange("p (r l m) -> p r l m", r=2, l=2)]
        at_out = view(10, 2, f16).rearrange("p (c m l w) -> p c m l w", c=NCH, m=MC, l=2)
        at_in = view(8, 4, f16).rearrange("p (c s m l w) -> p c s m l w", c=NCH, s=2, m=MC, l=2)
        t_bcast = view(4, 2).rearrange("p (h m) -> p h m", h=HEADS)
        feats = view(6, 1).rearrange("p (b d) -> p b d", d=D)
        mask = [view(2 + k, 1) for k in range(2)]
        biased = [view(7 + k / KV, 1 / KV) for k in range(4)]
        prob = [[view(8 + 2 * k + h, 1) for h in range(HEADS)] for k in range(2)]
        pt = [[view(1 + (2 * k + h) * 4 / NB, 4 / NB) for h in range(HEADS)] for k in range(2)]
        w0_sb = view(3, 1 / NB)
        win_sb, wout_sb, w1_sb, w2_sb, w3_sb, b1_b, b2_b = (
            view(7 + k / NB, 1 / NB) for k in range(7))
        neigh_b = view(7 + 8 / NB, 2 / NB).rearrange("p (h m) -> p h m", h=HEADS)

        ident = sb("ident", [P, P])
        w0t = sb("w0t", [P, P])
        b0_b = sb("b0_b", [P, P])
        b3_b = b0_b
        self_col = sb("self_col", [P, HEADS])
        a_cols = sb("a_cols", [P, 2])
        al = sb("al", [P, 2])
        half_neg = sb("half_neg", [P, NB])
        row_part = sb("row_part", [P, NB, NCH])
        col_part = sb("col_part", [P, NB, NS])
        rows = sb("rows", [P, NB])
        cols = sb("cols", [P, NB])
        inv_rows = sb("inv_rows", [P, NB])
        inv_cols = sb("inv_cols", [P, NB])
        d_nat = sb("d_nat", [P, NB])
        guard = sb("guard", [P, NB])
        inv0 = sb("inv0", [P, 4, 2])
        stage_a = sb("stage_a", [P, QW])
        stage_b = sb("stage_b", [P, QW])
        u_t = sb("u_t", [P, Q, D])
        v_t = sb("v_t", [P, Q, D])
        x1_st = sb("x1_st", [P, 2, 2, D], f16)
        stats = sb("stats", [P, Q, 6])
        mv = sb("mv", [P, Q, 2])
        var_e = sb("var_e", [P, Q])
        rstd = sb("rstd", [P, Q])
        s_nat = sb("s_nat", [P, NB, HEADS])
        row_max = sb("row_max", [P, HEADS, KV])
        neg_max = sb("neg_max", [P, 2, HEADS])
        row_sum = sb("row_sum", [P, NB, HEADS])
        inv_sum = sb("inv_sum", [P, HEADS])
        moment = sb("moment", [P, 1])

        ps = ctx.enter_context(nc.psum_tensor("ps", [P, 8 * 512], f32))
        bank = [ps[:, k * 512:(k + 1) * 512] for k in range(8)]
        tp_f = bank[0:4]
        ax_f = bank[4]
        atx_f = bank[5:7]
        ep_f = bank[7]
        acc = bank[0:2]
        ep = bank[2:6]
        leak_ps = [ps[:, k * 1024:k * 1024 + VW] for k in range(2)]
        tp_j = bank[4:6]
        av_j = bank[6]
        o_j = bank[7]

        def sem(name):
            return ctx.enter_context(nc.semaphore(name))

        s_const = sem("const_loaded")
        s_ident = sem("ident_ready")
        s_pool = sem("pool_setup")
        s_w0t = sem("w0t_transposed")
        s_set = sem("dve_setup")
        s_x0 = sem("x0_split")
        a_loaded = [sem(f"a_loaded{c}") for c in range(NCH)]
        at_stored = [sem(f"at_stored{c}") for c in range(NCH)]
        t_done, hi_done, lo_done = sem("a_transposed"), sem("at_hi"), sem("at_lo")
        sp_hi, sp_lo = sem("split_hi"), sem("split_lo")
        ax_done, qt_done = sem("ax_done"), sem("ax_taken")
        x0s_done, x0t_done, x0e_done = sem("x0_scaled"), sem("x0_transposed"), sem("x0t_taken")
        e1_done, var_f, rstd_f, x1_done, op1_done = (
            sem(n) for n in ("e1_done", "var_f", "rstd_f", "x1_done", "op1_done"))
        atx_done, atx_added = sem("atx_done"), sem("atx_added")
        ADDED_0 = 2
        link_f = sem("link_f")
        s_fin = sem("degrees_link")
        s_dpow = sem("degrees_pow")
        s_deg = sem("degrees_done")
        at_loaded = [sem(f"at_loaded{c}") for c in range(NCH)]
        at_used = sem("at_used")
        acc_done, acc_taken = sem("acc_done"), sem("acc_taken")
        ea_done = sem("ea_done")
        side_taken = sem("side_taken")
        var_q, rstd_q, mid_done = sem("var_q"), sem("rstd_q"), sem("mid_done")
        eb_done, eb_taken = sem("eb_done"), sem("eb_taken")
        ec_done, ops_done = sem("ec_done"), sem("ops_done")
        x_kept = sem("x_kept")
        link_q = sem("link_q")
        feat_t_taken, feat_done, ed_done, t_taken = (
            sem(n) for n in ("feat_t_taken", "feat_done", "ed_done", "t_taken"))
        s_late, s_neigh = sem("late_loaded"), sem("neigh_ready")
        m_loaded = [sem(f"m_loaded{k}") for k in range(2)]
        masked, bias_pool, bias_dve = sem("masked"), sem("biased_by_pool"), sem("biased_by_dve")
        leaked, scored = sem("leaked"), sem("scored")
        max_done, exp_done = sem("max_done"), sem("exp_done")
        tp_done = [sem(f"tp_done{h}") for h in range(HEADS)]
        tp_act, tp_dve = sem("tp_by_act"), sem("tp_by_dve")
        av_done, o_taken, o_done = sem("av_done"), sem("o_taken"), sem("o_done")
        var_j, rstd_j, y_done, y_out = sem("var_j"), sem("rstd_j"), sem("y_done"), [sem(f"y_out{k}") for k in range(2)]
        link_j = sem("link_j")

        EARLY, LATE = 4 + 2 * HEADS, 6 + 2 * HEADS

        class Count:

            def __init__(self, engine, name, first, step=1):
                self.engine, self.step = engine, step
                self.reg = engine.alloc_register(name)
                engine.reg_mov(self.reg, first)

            def wait(self, sem):
                self.engine.wait_ge(sem, self.reg)
                self.engine.reg_add(self.reg, self.reg, self.step)

        block = ctx.enter_context(nc.Block())

        @block.sync
        def _(sp):
            def load_a(s, c):
                sp.dma_start(a_in[:, c], adj[ds(s * W, W), c * CW:(c + 1) * CW]
                             .rearrange("(r p) m -> p r m", p=P)).then_inc(a_loaded[c], 16)

            early = [(x_nat, x_in.rearrange("(b p) d -> p b d", p=P)), (w0_sb, w0),
                     (al[:, 0:1], alpha.partition_broadcast(P)), (b0_b[:], b0.partition_broadcast(P))]
            for h in range(HEADS):
                early.append((a_cols[h * C:(h + 1) * C, 0:1], a_self[h].unsqueeze(1)))
                early.append((a_cols[h * C:(h + 1) * C, 1:2], a_neigh[h].unsqueeze(1)))
            assert len(early) == EARLY
            load_a(0, 0)
            for to, of in early:
                sp.dma_start(to, of).then_inc(s_const, 16)
            for c in range(1, NCH):
                load_a(0, c)

            def super_f(s, last=False):
                for c in range(NCH):
                    sp.wait_ge(lo_done, s * J + (c + 1) * SPC)
                    sp.dma_start(at_dram[ds(s, 1), c].rearrange("o p x -> (o p) x"),
                                 at_out[:, c].rearrange("p m l w -> p (m l w)")).then_inc(at_stored[c], 16)
                    if not last:
                        sp.wait_ge(sp_lo, s * NCH + c + 1)
                        load_a(s + 1, c)

            super_f(0)
            with sp.Fori(1, NS - 1) as s:
                super_f(s)
            super_f(NS - 1, last=True)

            def load_at(q, c):
                sp.dma_start(at_in[:, c].rearrange("p s m l w -> p s (m l w)"),
                             at_dram[ds(2 * q, 2), c].rearrange("s p x -> p s x")).then_inc(at_loaded[c], 16)

            sp.wait_ge(atx_done, U3 * (NS - 1))
            for c in range(2):
                sp.wait_ge(at_stored[c], 16 * NS)
                load_at(0, c)
            sp.wait_ge(ax_done, J * NS)
            for c in range(NCH):
                sp.wait_ge(at_stored[c], 16 * NS)
            for c in range(2, NCH):
                load_at(0, c)
            sp.wait_ge(atx_done, U3 * NS)
            late = [(win_sb, w_in), (wout_sb, w_out), (w1_sb, w1), (w2_sb, w2),
                    (b1_b, b1.partition_broadcast(P)), (b2_b, b2.partition_broadcast(P))]
            for h in range(HEADS):
                late.append((w3_sb[:, h * C:(h + 1) * C], w3[h]))
                late.append((b3_b[:, h * C:(h + 1) * C], b3[h].partition_broadcast(P)))
            assert len(late) == LATE
            for to, of in late:
                sp.dma_start(to, of).then_inc(s_late, 16)

            for ph in range(3):
                with sp.Fori(1 if ph == 0 else 0, NQ) as q:
                    for c in range(NCH):
                        sp.wait_ge(at_used, (ph * NQ + q - 1) * NCH + c + 1)
                        load_at(q, c)

            def load_mask(b, k):
                sp.dma_start(mask[k], adj[ds(b * P, P), :]).then_inc(m_loaded[k], 16)

            def rows_out(b, k):
                sp.wait_ge(y_done, b + 1)
                sp.dma_start(out[ds(b * P, P), :], v_t[:, k, :]).then_inc(y_out[k], 16)

            sp.wait_ge(at_used, 2 * NQ * NCH)
            load_mask(0, 0)
            sp.wait_ge(at_used, 3 * NQ * NCH)
            load_mask(1, 1)
            for b in range(2):
                sp.wait_ge(scored, (b + 1) * HEADS * KV)
                load_mask(b + 2, b)
            with sp.Fori(1, NB // 2 - 1) as it:
                for k in range(2):
                    b = 2 * it + k
                    sp.wait_ge(scored, (b + 1) * HEADS * KV)
                    load_mask(b + 2, k)
                    rows_out(b - 2, k)
            for b in range(NB - 4, NB):
                rows_out(b, b % 2)
            for k in range(2):
                sp.wait_ge(y_out[k], 16 * (NB // 2))

        @block.gpsimd
        def _(pool):
            nc.gpsimd.memset(ident[:], 0.0).then_inc(s_pool, 1)
            nc.gpsimd.memset(half_neg[:], -0.5).then_inc(s_pool, 1)
            pool.wait_ge(s_pool, 2)
            nc.gpsimd.affine_select(out=ident[:], in_=ident[:], compare_op=ALU.not_equal, fill=1.0, base=0,
                                    pattern=[[-1, P]], channel_multiplier=1).then_inc(s_ident, 1)

            def rsqrt_f(s):
                pool.wait_ge(var_f, s + 1)
                nc.gpsimd.tensor_tensor(rstd[:, 0:2], var_e[:, 0:2], half_neg[:, 0:2], ALU.pow).then_inc(rstd_f, 1)

            def super_f(s, par, first=False):
                if not first:
                    rsqrt_f(s - 1)
                for c in range(NCH):
                    pool.wait_ge(sp_hi, (s * NCH + c + 1) * 2)
                    cc = slice(c * CW, (c + 1) * CW)
                    nc.gpsimd.tensor_tensor(split[par][:, :, 1, cc], a_in[:, c], split[par][:, :, 0, cc],
                                            ALU.subtract).then_inc(sp_lo, 1)

            super_f(0, 0, first=True)
            with pool.Fori(0, (NS - 2) // 2) as it:
                for k in range(2):
                    super_f(2 * it + 1 + k, (1 + k) % 2)
            super_f(NS - 1, 1)
            rsqrt_f(NS - 1)
            pool.wait_ge(s_fin, 5)
            nc.gpsimd.tensor_tensor(d_nat[:], cols[:], half_neg[:], ALU.pow).then_inc(s_dpow, 1)

            for ph, lots in ((0, NQ), (2, NQ)):
                with pool.Fori(0, lots) as q:
                    pool.wait_ge(var_q, (NQ if ph else 0) + q + 1)
                    nc.gpsimd.tensor_tensor(rstd[:], var_e[:], half_neg[:, 0:Q], ALU.pow).then_inc(rstd_q, 1)

            def bias_piece(b, par, i):
                h, k = divmod(i, KV)
                vs = slice(k * VW, (k + 1) * VW)
                piece = mask[par][:, vs]
                if h == 0:
                    nc.gpsimd.tensor_scalar(piece, piece, -1.0, NEG_MASK, ALU.add, ALU.mult).then_inc(masked, 1)
                if i in BIAS_BY_DVE:
                    return
                pool.wait_ge(masked, b * KV + (k + 1 if h == 0 else KV))
                if not (isinstance(b, int) and b == 0 and i < 4):
                    pool.wait_ge(scored, b * PIECES + i - 3)
                nc.gpsimd.tensor_tensor(biased[i % 4], piece, t_bcast[:, h, vs], ALU.add).then_inc(bias_pool, 1)

            def block_j(b, par, rsqrt_of=None):
                loads[par].wait(m_loaded[par])
                for i in range(PIECES):
                    bias_piece(b, par, i)
                    if i == 5 and rsqrt_of is not None:
                        rsqrt_j(rsqrt_of)

            def rsqrt_j(b):
                pool.wait_ge(var_j, b + 1)
                nc.gpsimd.tensor_tensor(rstd[:, 0:1], var_e[:, 0:1], half_neg[:, 0:1], ALU.pow).then_inc(rstd_j, 1)

            loads = [Count(nc.gpsimd, f"mask_loads{k}", 16, 16) for k in range(2)]
            pool.wait_ge(t_taken, NQ)
            for b in range(2):
                block_j(b, b)
            with pool.Fori(1, NB // 2) as it:
                for k in range(2):
                    block_j(2 * it + k, k, rsqrt_of=2 * it + k - 2)
            rsqrt_j(NB - 2)
            rsqrt_j(NB - 1)

        @block.scalar
        def _(act):
            act.wait_ge(s_set, 1)

            def hi_parts(s, j):
                c, jj = divmod(j, SPC)
                act.wait_ge(t_done, s * J + j + 1)
                if jj == 0 and not (isinstance(s, int) and s == 0):
                    act.wait_ge(at_stored[c], 16 * s)
                    act.wait_ge(ax_done, (s - 1) * J + (c + 1) * SPC)
                for k in range(2):
                    op = nc.scalar.activation(at_out[:, c, 2 * jj + k, 0, :], tp_f[j % 4][:, k * W:(k + 1) * W],
                                              ACT.Copy, accum_out=col_part[:, 2 * j + k, ds(s, 1)])
                op.then_inc(hi_done, 1)

            def split_hi(s, par, c, r):
                act.wait_ge(a_loaded[c], 16 * (s + 1))
                nc.scalar.activation(split[par][:, r, 0, c * CW:(c + 1) * CW], a_in[:, c, r, :], ACT.Copy,
                                     accum_out=row_part[:, ds(2 * s + r, 1), c]).then_inc(sp_hi, 1)

            def super_f(s, par, first=False):
                for j in range(J):
                    hi_parts(s, j)
                    if j == min(SPLIT) and not first:
                        act.wait_ge(atx_added, ADDED_0 + K3 * (s - 1))
                    for c, r in SPLIT.get(j, []):
                        split_hi(s, par, c, r)
                    if j == J_NORM and not first:
                        keep_x1(s - 1)
                    if j == J_X0:
                        if not first:
                            act.wait_ge(qt_done, s)
                        nc.scalar.activation(u_x0, x_nat[:, ds(2 * s, 2), :], ACT.Copy,
                                             scale=al[:, 1:2]).then_inc(x0s_done, 1)
                    if j == J_X0 + 1:
                        act.wait_ge(x0t_done, s + 1)
                        nc.scalar.activation(stage_b[:, 0:W], ep_f[:, 0:W], ACT.Copy).then_inc(x0e_done, 1)

            def keep_x1(s):
                act.wait_ge(x1_done, s + 1)
                nc.scalar.activation(op_odd[:, ds(2 * s, 2)], x1_st[:], ACT.Copy).then_inc(op1_done, 1)

            u_x0 = v_t[:, 2:4, :]
            super_f(0, 0, first=True)
            with act.Fori(0, (NS - 2) // 2) as it:
                for k in range(2):
                    super_f(2 * it + 1 + k, (1 + k) % 2)
            super_f(NS - 1, 1)
            keep_x1(NS - 1)

            def take_acc(t, half):
                act.wait_ge(at_used, (t + 1) * NCH)
                nc.scalar.activation(stage_a[:], acc[half][:], ACT.Copy).then_inc(acc_taken, 1)

            def take_eb(t):
                act.wait_ge(eb_done, t + 1)
                nc.scalar.activation(stage_b[:], ep[1][:], ACT.Copy).then_inc(eb_taken, 1)

            act.wait_ge(atx_added, ADDED_0 + NS * K3)
            with act.Fori(0, NQ // 2) as it:
                for k in range(2):
                    q = 2 * it + k
                    take_acc(q, k)
                    nc.scalar.activation(stage_b[:], at_x1[:, ds(q * QW, QW)], ACT.Copy).then_inc(side_taken, 1)
                    take_eb(q)
            with act.Fori(0, NQ // 2) as it:
                for k in range(2):
                    t = NQ + 2 * it + k
                    take_acc(t, k)
                    take_eb(t)
            with act.Fori(0, NQ // 2) as it:
                for k in range(2):
                    q = 2 * it + k
                    take_acc(2 * NQ + q, k)
                    take_eb(2 * NQ + q)
                    act.wait_ge(ec_done, 2 * NQ + q + 1)
                    nc.scalar.activation(stage_a[:], ep[2][:], ACT.Copy).then_inc(feat_t_taken, 1)
                    act.wait_ge(ed_done, q + 1)
                    for h in range(HEADS):
                        nc.scalar.activation(t_bcast[:, h, ds(q * QW, QW)], ep[h][:], ACT.Copy, scale=LEAK)
                    nc.scalar.activation(s_nat[:, ds(q * Q, Q), :],
                                         ep[3][:, 0:Q * HEADS].rearrange("p (r h) -> p r h", h=HEADS),
                                         ACT.Copy, scale=1.0 - LEAK).then_inc(t_taken, 1)

            def leak(b, i):
                h, k = divmod(i, KV)
                if not (isinstance(b, int) and b == 0 and i < 2):
                    pieces_scored.wait(scored)
                nc.scalar.activation(leak_ps[i % 2], t_bcast[:, h, k * VW:(k + 1) * VW], ACT.Relu,
                                     bias=s_nat[:, ds(b, 1), h], scale=(1.0 - LEAK) / LEAK).then_inc(leaked, 1)

            def expo(b, par, h):
                act.wait_ge(max_done, b * HEADS + h + 1)
                nc.scalar.activation(prob[par][h], prob[par][h], ACT.Exp, bias=neg_max[:, par, h:h + 1],
                                     accum_out=row_sum[:, ds(b, 1), h]).then_inc(exp_done, 1)

            def take_tp(b, g):
                act.wait_ge(tp_done[0], b * G4 + g + 1)
                if not (isinstance(b, int) and b == 0 and g < 2):
                    act.wait_ge(av_done, b * G4 + g - 1)
                nc.scalar.activation(pt[g % 2][0], tp_j[0], ACT.Copy).then_inc(tp_act, 1)

            def take_out(b):
                act.wait_ge(av_done, (b + 1) * G4)
                if not (isinstance(b, int) and b == 0):
                    act.wait_ge(o_done, b)
                nc.scalar.activation(stage_a[:, 0:P], av_j[:, 0:P], ACT.Copy).then_inc(o_taken, 1)

            def block_j(b, par, first=False, last=False):
                for n, step in enumerate(ACT_PLAN.split()):
                    what, i = step[0], int(step[1:])
                    if what == "L" and not last:
                        leak(b + 1, i)
                    if what == "X" and not last:
                        expo(b + 1, 1 - par, i)
                    if what == "T":
                        take_tp(b, i)
                    if n == 1 and not first:
                        take_out(b - 1)

            pieces_scored = Count(nc.scalar, "pieces_scored", 1)
            act.wait_ge(t_taken, NQ)
            for i in range(HEADS * KV):
                leak(0, i)
            for h in range(HEADS):
                expo(0, 0, h)
            block_j(0, 0, first=True)
            block_j(1, 1)
            with act.Fori(1, NB // 2 - 1) as it:
                for k in range(2):
                    block_j(2 * it + k, k)
            block_j(NB - 2, 0)
            block_j(NB - 1, 1, last=True)
            take_out(NB - 1)

        @block.vector
        def _(dve):
            dve.wait_ge(s_const, 16 * EARLY)
            nc.vector.tensor_scalar(al[:, 1:2], al[:, 0:1], -1.0, 1.0, ALU.mult, ALU.add).then_inc(s_set, 1)
            nc.vector.tensor_copy(op_even[:, :, 0, :], x_nat).then_inc(s_set, 1)
            nc.vector.memset(self_col[:], 0.0).then_inc(atx_added, ADDED_0)
            nc.vector.memset(at_x1, 0.0).then_inc(s_set, 1)
            dve.wait_ge(s_set, 3)
            nc.vector.tensor_tensor(op_even[:, :, 1, :], x_nat, op_even[:, :, 0, :], ALU.subtract).then_inc(s_x0, 1)
            for h in range(HEADS):
                hc = slice(h * C, (h + 1) * C)
                nc.vector.tensor_copy(self_col[hc, h:h + 1], a_cols[hc, 0:1])
            dve.wait_ge(s_w0t, 1)
            nc.vector.tensor_copy(w0t[:], ep_f[:, 0:P]).then_inc(s_set, 1)

            def lo_parts(s, j):
                c, jj = divmod(j, SPC)
                dve.wait_ge(hi_done, s * J + j + 1)
                nc.vector.tensor_tensor(at_out[:, c, 2 * jj:2 * jj + 2, 1, :],
                                        tp_f[j % 4][:].rearrange("p (m w) -> p m w", m=2),
                                        at_out[:, c, 2 * jj:2 * jj + 2, 0, :], ALU.subtract).then_inc(lo_done, 1)

            def chain(base, counter):
                at = [base]

                def link(op):
                    at[0] = at[0] + 1
                    op.then_inc(counter, 1)
                    dve.wait_ge(counter, at[0])
                return link

            LINKS = 14

            def take_ax(s):
                link = chain(s * LINKS, link_f)
                dve.wait_ge(sp_hi, (s + 1) * NCH * 2)
                link(nc.vector.tensor_reduce(rows[:, ds(2 * s, 2)], row_part[:, ds(2 * s, 2), :], AX.X, ALU.add))
                link(nc.vector.tensor_scalar(inv0[:, 0, :], rows[:, ds(2 * s, 2)], al[:, 0:1], al[:, 1:2],
                                             ALU.mult, ALU.add))
                link(nc.vector.tensor_scalar(inv0[:, 1, :], inv0[:, 0, :], 0.0, None, ALU.is_equal))
                link(nc.vector.tensor_tensor(inv0[:, 2, :], inv0[:, 0, :], inv0[:, 1, :], ALU.add))
                link(nc.vector.reciprocal(inv0[:, 3, :], inv0[:, 2, :]))
                link(nc.vector.tensor_tensor(inv0[:, 0, :], inv0[:, 3, :], inv0[:, 1, :], ALU.mult))
                link(nc.vector.tensor_tensor(inv0[:, 3, :], inv0[:, 3, :], inv0[:, 0, :], ALU.subtract))
                dve.wait_ge(ax_done, (s + 1) * J)
                dve.wait_ge(x0e_done, s + 1)
                nc.vector.scalar_tensor_tensor(out=stage_a[:, 0:W], in0=ax_f[:, 0:W], scalar=al[:, 0:1],
                                               in1=stage_b[:, 0:W], op0=ALU.mult, op1=ALU.add).then_inc(qt_done, 1)

            def stats_f(s):
                link = chain(s * LINKS + 7, link_f)
                dve.wait_ge(e1_done, s + 1)
                for r in range(2):
                    op = nc.vector.scalar_tensor_tensor(out=u_t[:, r, :], in0=ep_f[:, r * P:(r + 1) * P],
                                                        scalar=inv0[:, 3, r:r + 1], in1=b0_b[:],
                                                        op0=ALU.mult, op1=ALU.add)
                link(op)
                link(nc.vector.scalar_tensor_tensor(out=u_t[:, 0:2, :], in0=u_t[:, 0:2, :], scalar=0.0,
                                                    in1=x_nat[:, ds(2 * s, 2), :], op0=ALU.max, op1=ALU.add))
                for r in range(2):
                    op = nc.vector.bn_stats(stats[:, r, :], u_t[:, r, :])
                link(op)
                nc.vector.memset(moment[:], 0.0)
                for r in range(2):
                    op = nc.vector.bn_aggr(mv[:, r, :], stats[:, r, :])
                link(op)
                nc.vector.tensor_scalar(var_e[:, 0:2], mv[:, 0:2, 1], EPS, None, ALU.add).then_inc(var_f, 1)

            def norm_f(s):
                link = chain(s * LINKS + 11, link_f)
                dve.wait_ge(rstd_f, s + 1)
                for r in range(2):
                    op = nc.vector.tensor_scalar(v_t[:, r, :], u_t[:, r, :], mv[:, r, 0:1], rstd[:, r:r + 1],
                                                 ALU.subtract, ALU.mult)
                link(op)
                dve.wait_ge(x0s_done, s + 1)
                if not (isinstance(s, int) and s == 0):
                    dve.wait_ge(atx_done, U3 * s)
                    dve.wait_ge(op1_done, s)
                link(nc.vector.tensor_scalar(x_nat[:, ds(2 * s, 2), :], v_t[:, 0:2, :], 1.0, None, ALU.mult))
                link(nc.vector.tensor_copy(x1_st[:, :, 0, :], v_t[:, 0:2, :]))
                nc.vector.tensor_tensor(x1_st[:, :, 1, :], v_t[:, 0:2, :], x1_st[:, :, 0, :],
                                        ALU.subtract).then_inc(x1_done, 1)

            def add_atx(s, k):
                n = s * K3 + k
                dve.wait_ge(atx_done, s * U3 + 2 * k + 2)
                if not (isinstance(s, int) and s == 0):
                    dve.wait_ge(atx_added, ADDED_0 + n - K3 + 1)
                piece = at_x1[:, k * 512:(k + 1) * 512]
                nc.vector.tensor_tensor(piece, atx_f[k % 2][:], piece, ALU.add).then_inc(atx_added, 1)

            def super_f(s, first=False):
                for j in range(J):
                    lo_parts(s, j)
                    if first:
                        continue
                    if j == 1:
                        take_ax(s - 1)
                    if j == J_STAT:
                        stats_f(s - 1)
                    if j == J_NORM:
                        norm_f(s - 1)
                    for u in units_at(j):
                        if u % 2:
                            add_atx(s - 1, u // 2)

            super_f(0, first=True)
            super_f(1)
            with dve.Fori(2, NS) as s:
                super_f(s)
            take_ax(NS - 1)
            stats_f(NS - 1)
            norm_f(NS - 1)
            for k in range(K3):
                add_atx(NS - 1, k)

            n_fin = [0]

            def link(op):
                n_fin[0] += 1
                op.then_inc(s_fin, 1)
                dve.wait_ge(s_fin, n_fin[0])

            def where_positive(to, of):
                link(nc.vector.tensor_scalar(guard[:], of, 0.0, None, ALU.is_gt))
                link(nc.vector.tensor_tensor(to, of, guard[:], ALU.mult))
                link(nc.vector.tensor_scalar(inv_cols[:], guard[:], -1.0, 1.0, ALU.mult, ALU.add))
                link(nc.vector.tensor_tensor(to, to, inv_cols[:], ALU.add))

            link(nc.vector.tensor_scalar(inv_rows[:], rows[:], 1.0, None, ALU.add))
            where_positive(cols[:], inv_rows[:])
            assert n_fin[0] == 5
            dve.wait_ge(s_dpow, 1)
            link(nc.vector.tensor_tensor(d_nat[:], d_nat[:], guard[:], ALU.mult))
            dve.wait_ge(hi_done, NS * J)
            link(nc.vector.tensor_reduce(cols[:], col_part[:], AX.X, ALU.add))
            where_positive(inv_rows[:], rows[:])
            link(nc.vector.reciprocal(inv_rows[:], inv_rows[:]))
            where_positive(rows[:], cols[:])
            link(nc.vector.reciprocal(inv_cols[:], rows[:]))
            dve.wait_ge(s_late, 16 * LATE)
            link(nc.vector.memset(neigh_b, 0.0))
            for h in range(HEADS):
                hc = slice(h * C, (h + 1) * C)
                op = nc.vector.tensor_copy(neigh_b[hc, h, :], a_cols[hc, 1:2].to_broadcast([C, P]))
            op.then_inc(s_neigh, 1)

            LG, LH, LI = 8, 5, 6

            def layernorm_in(link):
                for r in range(Q):
                    op = nc.vector.bn_stats(stats[:, r, :], u_t[:, r, :])
                link(op)
                nc.vector.memset(moment[:], 0.0)
                for r in range(Q):
                    op = nc.vector.bn_aggr(mv[:, r, :], stats[:, r, :])
                link(op)
                nc.vector.tensor_scalar(var_e[:], mv[:, :, 1], EPS, None, ALU.add).then_inc(var_q, 1)

            def layernorm_out(link, q, n, t):
                dve.wait_ge(rstd_q, n)
                for r in range(Q):
                    op = nc.vector.tensor_scalar(v_t[:, r, :], u_t[:, r, :], mv[:, r, 0:1], rstd[:, r:r + 1],
                                                 ALU.subtract, ALU.mult)
                op.then_inc(mid_done, 1)
                dve.wait_ge(mid_done, t + 1)
                link(nc.vector.tensor_scalar(x_nat[:, ds(Q * q, Q), :], v_t[:], 1.0, None, ALU.mult))

            def operands(link, q, t, to):
                dve.wait_ge(ec_done, t + 1)
                for r in range(Q):
                    op = nc.vector.tensor_scalar(u_t[:, r, :], ep[2][:, r * P:(r + 1) * P],
                                                 d_nat[:, ds(Q * q + r, 1)], None, ALU.mult)
                link(op)
                link(nc.vector.tensor_scalar(y_nat[:, ds(Q * q, Q), :], u_t[:], 1.0, None, ALU.mult))
                link(nc.vector.tensor_scalar(to[:, ds(Q * q, Q), 0, :], u_t[:], 1.0, None, ALU.mult))
                nc.vector.tensor_tensor(to[:, ds(Q * q, Q), 1, :], u_t[:], to[:, ds(Q * q, Q), 0, :],
                                        ALU.subtract).then_inc(ops_done, 1)
                dve.wait_ge(ops_done, t + 1)

            with dve.Fori(0, NQ) as q:
                link = chain(q * LG, link_q)
                dve.wait_ge(ea_done, q + 1)
                for r in range(Q):
                    op = nc.vector.scalar_tensor_tensor(out=u_t[:, r, :], in0=ep[0][:, r * P:(r + 1) * P],
                                                        scalar=inv_rows[:, ds(Q * q + r, 1)],
                                                        in1=x_nat[:, ds(Q * q + r, 1), :].rearrange("p o d -> p (o d)"),
                                                        op0=ALU.mult, op1=ALU.add)
                link(op)
                for r in range(Q):
                    op = nc.vector.scalar_tensor_tensor(out=u_t[:, r, :], in0=ep[3][:, r * P:(r + 1) * P],
                                                        scalar=inv_cols[:, ds(Q * q + r, 1)], in1=u_t[:, r, :],
                                                        op0=ALU.mult, op1=ALU.add)
                link(op)
                layernorm_in(link)
                layernorm_out(link, q, q + 1, q)
                operands(link, q, q, op_even)

            with dve.Fori(0, NQ) as q:
                link = chain(NQ * LG + q * LH, link_q)
                dve.wait_ge(ea_done, NQ + q + 1)
                yq = y_nat[:, ds(Q * q, Q), :]
                link(nc.vector.tensor_tensor(u_t[:], ep[0][:].rearrange("p (r d) -> p r d", r=Q), yq, ALU.add))
                for r in range(Q):
                    op = nc.vector.scalar_tensor_tensor(out=v_t[:, r, :], in0=u_t[:, r, :],
                                                        scalar=d_nat[:, ds(Q * q + r, 1)], in1=b1_b[:],
                                                        op0=ALU.mult, op1=ALU.add)
                link(op)
                nc.vector.tensor_scalar(v_t[:], v_t[:], 0.0, None, ALU.max).then_inc(mid_done, 1)
                operands(link, q, NQ + q, op_odd)

            with dve.Fori(0, NQ) as q:
                link = chain(NQ * (LG + LH) + q * LI, link_q)
                t = 2 * NQ + q
                dve.wait_ge(ea_done, t + 1)
                yq = y_nat[:, ds(Q * q, Q), :]
                link(nc.vector.tensor_tensor(u_t[:], ep[0][:].rearrange("p (r d) -> p r d", r=Q), yq, ALU.add))
                for r in range(Q):
                    op = nc.vector.scalar_tensor_tensor(out=u_t[:, r, :], in0=u_t[:, r, :],
                                                        scalar=d_nat[:, ds(Q * q + r, 1)], in1=b2_b[:],
                                                        op0=ALU.mult, op1=ALU.add)
                link(op)
                link(nc.vector.tensor_tensor(u_t[:], u_t[:], x_nat[:, ds(Q * q, Q), :], ALU.add))
                layernorm_in(link)
                layernorm_out(link, q, NQ + q + 1, t)
                dve.wait_ge(feat_done, q + 1)
                nc.vector.tensor_scalar(feats[:, ds(Q * q, Q), :], ep[3][:].rearrange("p (r d) -> p r d", r=Q), 1.0, None,
                                        ALU.mult).then_inc(ops_done, 1)

            def score(b, par, i):
                h, k = divmod(i, KV)
                vs = slice(k * VW, (k + 1) * VW)
                if k == 0 and not (isinstance(b, int) and b < 2):
                    dve.wait_ge(tp_done[h], (b - 1) * G4)
                if i in BIAS_BY_DVE:
                    n = b * len(BIAS_BY_DVE) + BIAS_BY_DVE.index(i) + 1
                    dve.wait_ge(masked, b * KV + (k + 1 if h == 0 else KV))
                    nc.vector.tensor_tensor(biased[i % 4], mask[par][:, vs], t_bcast[:, h, vs],
                                            ALU.add).then_inc(bias_dve, 1)
                    dve.wait_ge(bias_dve, n)
                else:
                    mine = [z for z in range(PIECES) if z not in BIAS_BY_DVE]
                    dve.wait_ge(bias_pool, b * len(mine) + mine.index(i) + 1)
                pieces_leaked.wait(leaked)
                nc.vector.tensor_tensor_reduce(out=prob[par][h][:, vs], in0=leak_ps[i % 2], in1=biased[i % 4],
                                               scale=1.0, scalar=LOWEST, op0=ALU.add, op1=ALU.max,
                                               accum_out=row_max[:, h, k:k + 1]).then_inc(scored, 1)

            def maximum(b, par, h):
                dve.wait_ge(scored, b * HEADS * KV + (h + 1) * KV)
                if not (isinstance(b, int) and b < 2):
                    dve.wait_ge(exp_done, (b - 1) * HEADS)
                nc.vector.tensor_reduce(neg_max[:, par, h:h + 1], row_max[:, h, :], AX.X, ALU.max,
                                        negate=True).then_inc(max_done, 1)

            def take_tp(b, g):
                for h in range(HEADS):
                    if h == 0 and g in BY_ACT:
                        continue
                    dve.wait_ge(tp_done[h], b * G4 + g + 1)
                    if not (isinstance(b, int) and b == 0 and g < 2):
                        dve.wait_ge(av_done, b * G4 + g - 1)
                    nc.vector.tensor_copy(pt[g % 2][h], tp_j[h]).then_inc(tp_dve, 1)

            LJ = 5

            def stats_j(b, par):
                link = chain(b * LJ, link_j)
                dve.wait_ge(o_done, b + 1)
                link(nc.vector.reciprocal(inv_sum[:], row_sum[:, ds(b, 1), :].rearrange("p o h -> p (o h)")))
                for h in range(HEADS):
                    hc = slice(h * C, (h + 1) * C)
                    op = nc.vector.scalar_tensor_tensor(out=u_t[:, 0, hc], in0=o_j[:, hc], scalar=inv_sum[:, h:h + 1],
                                                        in1=b3_b[:, hc], op0=ALU.mult, op1=ALU.add)
                link(op)
                link(nc.vector.scalar_tensor_tensor(out=u_t[:, 0, :], in0=u_t[:, 0, :], scalar=0.0,
                                                    in1=x_nat[:, ds(b, 1), :].rearrange("p o d -> p (o d)"),
                                                    op0=ALU.max, op1=ALU.add))
                link(nc.vector.bn_stats(stats[:, 0, :], u_t[:, 0, :]))
                nc.vector.memset(moment[:], 0.0)
                link(nc.vector.bn_aggr(mv[:, 0, :], stats[:, 0, :]))
                nc.vector.tensor_scalar(var_e[:, 0:1], mv[:, 0, 1:2], EPS, None, ALU.add).then_inc(var_j, 1)

            def norm_j(b, n, par):
                dve.wait_ge(rstd_j, b + 1)
                if not (isinstance(n, int) and n == 0):
                    dve.wait_ge(y_out[par], 16 * n)
                nc.vector.tensor_scalar(v_t[:, par, :], u_t[:, 0, :], mv[:, 0, 0:1], rstd[:, 0:1],
                                        ALU.subtract, ALU.mult).then_inc(y_done, 1)

            def block_j(b, n, par, first=False, last=False):
                plan = DVE_PLAN.split()
                for at, step in enumerate(plan):
                    what, i = step[0], int(step[1:])
                    if what == "S" and not last:
                        score(b + 1, 1 - par, i)
                        if i == KV:
                            maximum(b + 1, 1 - par, 0)
                    if what == "M" and not last:
                        maximum(b + 1, 1 - par, 1)
                    if what == "V":
                        take_tp(b, i)
                    if at == plan.index("V1") + 1 and not first:
                        stats_j(b - 1, 1 - par)
                if not first:
                    norm_j(b - 1, n - (1 - par), 1 - par)

            pieces_leaked = Count(nc.vector, "pieces_leaked", 1)
            for i in range(HEADS * KV):
                score(0, 0, i)
                if i % KV == KV - 1:
                    maximum(0, 0, i // KV)
            block_j(0, 0, 0, first=True)
            block_j(1, 0, 1)
            with dve.Fori(1, NB // 2 - 1) as it:
                for k in range(2):
                    block_j(2 * it + k, it, k)
            block_j(NB - 2, NB // 2 - 1, 0)
            block_j(NB - 1, NB // 2 - 1, 1, last=True)
            stats_j(NB - 1, 1)
            norm_j(NB - 1, NB // 2 - 1, 1)

        @block.tensor
        def _(pe):
            pe.wait_ge(s_ident, 1)
            pe.wait_ge(s_const, 16 * EARLY)
            nc.tensor.transpose(ep_f[:, 0:P], w0_sb, ident[:]).then_inc(s_w0t, 1)

            def transposes(s, j):
                c, jj = divmod(j, SPC)
                if jj == 0:
                    pe.wait_ge(a_loaded[c], 16 * (s + 1))
                if not (isinstance(s, int) and s == 0 and j < 4):
                    pe.wait_ge(lo_done, s * J + j - 3)
                for k in range(2):
                    for r in range(2):
                        m = (2 * jj + k) * P
                        op = nc.tensor.transpose(tp_f[j % 4][:, k * W + r * P:k * W + (r + 1) * P],
                                                 a_in[:, c, r, m:m + P], ident[:])
                op.then_inc(t_done, 1)

            def ax_step(s, j):
                c, jj = divmod(j, SPC)
                pe.wait_ge(lo_done, s * J + j + 1)
                if j == 0 and not (isinstance(s, int) and s == 0):
                    pe.wait_ge(qt_done, s)
                for k in range(2):
                    m = 2 * j + k
                    hi, lo = (at_out[:, c, 2 * jj + k, z, :] for z in range(2))
                    nc.tensor.matmul(ax_f[:, 0:W], op_even[:, m, 0, :], hi, start=(m == 0), stop=False)
                    nc.tensor.matmul(ax_f[:, 0:W], op_even[:, m, 0, :], lo, start=False, stop=False)
                    op = nc.tensor.matmul(ax_f[:, 0:W], op_even[:, m, 1, :], hi, start=False, stop=(m == NB - 1))
                op.then_inc(ax_done, 1)

            def layer0(s):
                pe.wait_ge(qt_done, s + 1)
                for r in range(2):
                    op = nc.tensor.matmul(ep_f[:, r * P:(r + 1) * P], stage_a[:, r * P:(r + 1) * P], w0t[:],
                                          start=True, stop=True)
                op.then_inc(e1_done, 1)

            def x0_transposed(s):
                pe.wait_ge(x0s_done, s + 1)
                if not (isinstance(s, int) and s == 0):
                    pe.wait_ge(var_f, s)
                for r in range(2):
                    op = nc.tensor.transpose(ep_f[:, r * P:(r + 1) * P], v_t[:, 2 + r, :], ident[:])
                op.then_inc(x0t_done, 1)

            def atx_unit(s, par, u):
                k, r = divmod(u, 2)
                if u == 0:
                    pe.wait_ge(x1_done, s + 1)
                if r == 0:
                    pe.wait_ge(sp_lo, s * NCH + ((k + 1) * 512 - 1) // CW + 1)
                    if not (isinstance(s, int) and s == 0 and k < 2):
                        pe.wait_ge(atx_added, ADDED_0 + s * K3 + k - 1)
                hi, lo = (split[par][:, r, z, k * 512:(k + 1) * 512] for z in range(2))
                nc.tensor.matmul(atx_f[k % 2], x1_st[:, r, 0, :], hi, start=(r == 0), stop=False)
                nc.tensor.matmul(atx_f[k % 2], x1_st[:, r, 0, :], lo, start=False, stop=False)
                nc.tensor.matmul(atx_f[k % 2], x1_st[:, r, 1, :], hi, start=False, stop=(r == 1)).then_inc(atx_done, 1)

            def super_f(s, par, first=False):
                for j in range(J):
                    transposes(s, j)
                    if j >= 2:
                        ax_step(s, j - 2)
                    elif not first:
                        ax_step(s - 1, J - 2 + j)
                    if j == J_E1 and not first:
                        layer0(s - 1)
                    if j == J_X0 + 1:
                        x0_transposed(s)
                    if not first:
                        for u in units_at(j):
                            atx_unit(s - 1, 1 - par, u)

            pe.wait_ge(s_set, 4)
            pe.wait_ge(s_x0, 1)
            super_f(0, 0, first=True)
            with pe.Fori(0, (NS - 2) // 2) as it:
                for k in range(2):
                    super_f(2 * it + 1 + k, (1 + k) % 2)
            super_f(NS - 1, 1)
            ax_step(NS - 1, J - 2)
            ax_step(NS - 1, J - 1)
            layer0(NS - 1)
            for u in range(U3):
                atx_unit(NS - 1, 1, u)

            def chunk(ph, q, half, c):
                t = ph * NQ + q
                y = (op_odd, op_even, op_odd)[ph]
                pe.wait_ge(at_loaded[c], 16 * (t + 1))
                if isinstance(q, int) and q == 0:
                    if ph == 0:
                        pe.wait_ge(op1_done, NS)
                    else:
                        pe.wait_ge(ops_done, (ph - 1) * NQ - (-(c + 1) * NQ // NCH))
                if c == 0 and not (isinstance(t, int) and t < 2):
                    pe.wait_ge(acc_taken, t - 1)
                for m in range(MC):
                    b = c * MC + m
                    hi, lo = (at_in[:, c, :, m, z, :] for z in range(2))
                    to = acc[half].rearrange("p (s w) -> p s w", s=2)
                    nc.tensor.matmul(to, y[:, b, 0, :], hi, start=(b == 0), stop=False)
                    nc.tensor.matmul(to, y[:, b, 0, :], lo, start=False, stop=False)
                    op = nc.tensor.matmul(to, y[:, b, 1, :], hi, start=False, stop=(b == NB - 1))
                op.then_inc(at_used, 1)

            def four(to, of, weights):
                for r in range(Q):
                    op = nc.tensor.matmul(to[:, r * P:(r + 1) * P], of[:, r * P:(r + 1) * P], weights,
                                          start=True, stop=True)
                return op

            def four_transposes(to, of):
                for r in range(Q):
                    op = nc.tensor.transpose(to[:, r * P:(r + 1) * P], of(r), ident[:])
                return op

            def epilogue_a(ph, q):
                t = ph * NQ + q
                pe.wait_ge(acc_taken, t + 1)
                if ph == 0:
                    pe.wait_ge(side_taken, q + 1)
                    four(ep[3], stage_b, wout_sb)
                    four(ep[0], stage_a, win_sb).then_inc(ea_done, 1)
                else:
                    if ph == 2 and not (isinstance(q, int) and q == 0):
                        pe.wait_ge(t_taken, q)
                    four_transposes(ep[0], lambda r: stage_a[:, r * P:(r + 1) * P]).then_inc(ea_done, 1)

            def epilogue_b(ph, q):
                pe.wait_ge(mid_done, ph * NQ + q + 1)
                four_transposes(ep[1], lambda r: v_t[:, r, :]).then_inc(eb_done, 1)

            def epilogue_c(ph, q):
                t = ph * NQ + q
                pe.wait_ge(eb_taken, t + 1)
                if not (isinstance(t, int) and t == 0):
                    pe.wait_ge(ops_done, t)
                if ph < 2:
                    four(ep[2], stage_b, (w1_sb, w2_sb)[ph]).then_inc(ec_done, 1)
                    return
                nc.tensor.matmul(ep[2], w3_sb, stage_b[:], start=True, stop=True).then_inc(ec_done, 1)
                four(ep[3], stage_b, w3_sb).then_inc(feat_done, 1)
                pe.wait_ge(feat_t_taken, q + 1)
                for h in range(HEADS):
                    nc.tensor.matmul(ep[h], neigh_b[:, h, :], stage_a[:], start=True, stop=True)
                pe.wait_ge(ops_done, t + 1)
                for r in range(Q):
                    op = nc.tensor.matmul(ep[3][:, r * HEADS:(r + 1) * HEADS], stage_a[:, r * P:(r + 1) * P],
                                          self_col[:], start=True, stop=True)
                op.then_inc(ed_done, 1)

            def quad(ph, q, half, before=None):
                chunk(ph, q, half, 0)
                if before:
                    epilogue_a(*before)
                chunk(ph, q, half, 1)
                if before:
                    epilogue_b(*before)
                chunk(ph, q, half, 2)
                if before:
                    epilogue_c(*before)
                chunk(ph, q, half, 3)

            quad(0, 0, 0)
            pe.wait_ge(s_late, 16 * LATE)
            pe.wait_ge(atx_added, ADDED_0 + NS * K3)
            quad(0, 1, 1, (0, 0))
            with pe.Fori(1, NQ // 2) as it:
                for k in range(2):
                    quad(0, 2 * it + k, k, (0, 2 * it + k - 1))
            for ph in (1, 2):
                if ph == 2:
                    pe.wait_ge(s_neigh, 1)
                quad(ph, 0, 0, (ph - 1, NQ - 1))
                quad(ph, 1, 1, (ph, 0))
                with pe.Fori(1, NQ // 2) as it:
                    for k in range(2):
                        quad(ph, 2 * it + k, k, (ph, 2 * it + k - 1))
            epilogue_a(2, NQ - 1)
            epilogue_b(2, NQ - 1)
            epilogue_c(2, NQ - 1)

            def taken(b, g, h):
                if h == 0 and g in BY_ACT:
                    pe.wait_ge(tp_act, b * len(BY_ACT) + BY_ACT.index(g) + 1)
                else:
                    per = HEADS * G4 - len(BY_ACT)
                    mine = [(gg, hh) for gg in range(G4) for hh in range(HEADS) if not (hh == 0 and gg in BY_ACT)]
                    assert len(mine) == per
                    pe.wait_ge(tp_dve, b * per + mine.index((g, h)) + 1)

            def tp_group(b, par, g):
                for h in range(HEADS):
                    if g == 0:
                        pe.wait_ge(exp_done, b * HEADS + h + 1)
                        if not (isinstance(b, int) and b == 0):
                            taken(b - 1, G4 - 1, h)
                    else:
                        taken(b, g - 1, h)
                    for k in range(4):
                        m = (4 * g + k) * P
                        op = nc.tensor.transpose(tp_j[h][:, k * P:(k + 1) * P], prob[par][h][:, m:m + P], ident[:])
                    op.then_inc(tp_done[h], 1)

            def av_group(b, g):
                for h in range(HEADS):
                    taken(b, g, h)
                if g == 0 and not (isinstance(b, int) and b == 0):
                    pe.wait_ge(o_taken, b)
                for k in range(4):
                    m = 4 * g + k
                    for h in range(HEADS):
                        hc = slice(h * C, (h + 1) * C)
                        op = nc.tensor.matmul(av_j[hc, 0:P], feats[:, m, hc], pt[g % 2][h][:, k * P:(k + 1) * P],
                                              start=(m == 0), stop=(m == NB - 1))
                op.then_inc(av_done, 1)

            def out_rows(b):
                pe.wait_ge(o_taken, b + 1)
                if not (isinstance(b, int) and b == 0):
                    pe.wait_ge(var_j, b)
                nc.tensor.transpose(o_j[:, 0:P], stage_a[:, 0:P], ident[:]).then_inc(o_done, 1)

            def block_j(b, par, first=False):
                for g in range(G4):
                    tp_group(b, par, g)
                    if g == 1 and not first:
                        out_rows(b - 1)
                    if g >= 1:
                        av_group(b, g - 1)
                av_group(b, G4 - 1)

            pe.wait_ge(ops_done, 3 * NQ)
            block_j(0, 0, first=True)
            block_j(1, 1)
            with pe.Fori(1, NB // 2) as it:
                for k in range(2):
                    block_j(2 * it + k, k)
            out_rows(NB - 1)


_INS = ["x", "adj", "L0_gnn_alpha", "L0_gnn_W", "L0_gnn_b", "L1_gnn_W_in", "L1_gnn_W_out", "L2_gnn_W1", "L2_gnn_b1",
        "L2_gnn_W2", "L2_gnn_b2", "L3_gnn_W", "L3_gnn_a_self", "L3_gnn_a_neigh", "L3_gnn_b"]


def kernel(**inputs):
    import numpy as _np
    import concourse.bacc as _bacc
    from concourse import mybir as _mybir
    from concourse.bass_utils import run_bass_kernel_spmd as _run

    nc = _bacc.Bacc("TRN2", target_bir_lowering=False, num_devices=1)
    arrays, args = {}, []
    for name in _INS:
        a = _np.ascontiguousarray(inputs[name])
        arrays[f"in_{name}"] = a
        args.append(nc.dram_tensor(f"in_{name}", a.shape, _mybir.dt.from_np(a.dtype), kind="ExternalInput").ap())
    shape = arrays["in_x"].shape
    args.append(nc.dram_tensor("out_0", shape, _mybir.dt.float32, kind="ExternalOutput").ap())
    graph_stack(nc, *args)
    r = _run(nc, [arrays], core_ids=[0])
    return r.results[0]["out_0"]
```

```python
import concourse.bass as bass
from concourse import mybir
from contextlib import ExitStack


def graph_stack(nc, x_in, adj, alpha, w0, b0, w_in, w_out, w1, b1, w2, b2, w3, a_self, a_neigh, b3, out):
    f32, f16 = mybir.dt.float32, mybir.dt.float16
    ALU = mybir.AluOpType
    ACT = mybir.ActivationFunctionType
    AX = mybir.AxisListType
    ds = bass.ds

    P = 128
    N, D = x_in.shape
    NB = N // P
    HEADS = w3.shape[0]
    C = w3.shape[2]
    EPS = 1e-5
    NEG_MASK = 1e10
    LEAK = 0.2
    LOWEST = -3.0e38

    NS = NB // 2
    NCH = 4
    MC = NB // NCH
    J = NB // 2
    SPC = J // NCH
    CW = MC * P
    W = 2 * P
    K3 = N // 512
    U3 = 2 * K3
    J_TAKE, J_DEG, J_E1, J_RELU, J_NORM = 1, 2, 3, 4, 8
    J_X0 = J // 2
    J_P3 = J_NORM + 2
    assert U3 == J
    SPLIT = {2: (0, 0), 4: (0, 1), 6: (1, 0), 8: (1, 1), 10: (2, 0), 11: (2, 1), 13: (3, 0), 14: (3, 1)}

    def unit_at(s, j):
        return (s - 1 if j >= J_P3 else s - 2), (j - J_P3) % J

    NQ = NB // 4
    Q = 4
    QW = Q * P

    KV = 4
    VW = N // KV
    G4 = NB // 4
    PIECES = HEADS * KV
    FUSED = [0, PIECES - 1]
    LEAKED = [i for i in range(PIECES) if i not in FUSED]
    ACT_PLAN = "L1 L2 O0 T00 T01 L3 T10 T11 L4 T20 T21 L5 T30 L6 T31 T40 X0 X1 T71"
    DVE_PLAN = "F0 F7 S0 S1 S2 S3 O0 S4 S5 S6 V41 S7 V50 V51 M0 N0 V60 V61 V70"
    BY_ACT = [(int(t[1]), int(t[2])) for t in ACT_PLAN.split() if t[0] == "T"]
    BY_DVE = [(int(t[1]), int(t[2])) for t in DVE_PLAN.split() if t[0] == "V"]
    assert sorted(BY_ACT + BY_DVE) == [(g, h) for g in range(G4) for h in range(HEADS)]

    at_dram = nc.dram_tensor("at_parts", [NS, NCH, P, MC * 2 * W], f16, kind="Internal").ap()

    ctx = ExitStack()
    with ctx:
        KB = 256
        block_kb = NB * P * 4 // 1024
        words = 12 * block_kb * KB
        arena = ctx.enter_context(nc.sbuf_tensor("arena", [P, words], f32))

        def view(at, size, dt=f32):
            v = arena[:, int(at * NB * P):int((at + size) * NB * P)]
            return v if dt is f32 else v.bitcast(dt)

        def sb(name, shape, dt=f32):
            return ctx.enter_context(nc.sbuf_tensor(name, shape, dt))

        x_nat = view(0, 1).rearrange("p (b d) -> p b d", d=D)
        at_x1 = view(1, 1)
        y_nat = view(1, 1).rearrange("p (b d) -> p b d", d=D)
        op_even = view(2, 1, f16).rearrange("p (b l d) -> p b l d", l=2, d=D)
        op_odd = view(3, 1, f16).rearrange("p (b l d) -> p b l d", l=2, d=D)
        a_in = view(4, 2).rearrange("p (c r m) -> p c r m", c=NCH, r=2)
        split = [view(8, 2, f16).rearrange("p (r l m) -> p r l m", r=2, l=2),
                 view(6, 2, f16).rearrange("p (r l m) -> p r l m", r=2, l=2)]
        at_out = view(10, 2, f16).rearrange("p (c m l w) -> p c m l w", c=NCH, m=MC, l=2)
        at_in = view(8, 4, f16).rearrange("p (c s m l w) -> p c s m l w", c=NCH, s=2, m=MC, l=2)
        t_bcast = view(4, 2).rearrange("p (h m) -> p h m", h=HEADS)
        feats = view(6, 1).rearrange("p (b d) -> p b d", d=D)
        mask = [view(2 + k, 1) for k in range(2)]
        biased = [view((7, 7.25, 1.5, 1.75)[k], VW / N) for k in range(4)]
        t_whole = [view(7.5 + k * VW / N, VW / N) for k in range(len(FUSED))]
        prob = [[view(8 + 2 * k + h, 1) for h in range(HEADS)] for k in range(2)]
        pt = [[view(1 + (2 * k + h) * 4 / NB, 4 / NB) for h in range(HEADS)] for k in range(2)]
        w0_sb = view(3, 1 / NB)
        win_sb, wout_sb, w1_sb, w2_sb, w3_sb, b1_b, b2_b = (
            view(7 + k / NB, 1 / NB) for k in range(7))
        neigh_b = view(7 + 8 / NB, 2 / NB).rearrange("p (h m) -> p h m", h=HEADS)

        ident = sb("ident", [P, P])
        w0t = sb("w0t", [P, P])
        b0_b = sb("b0_b", [P, P])
        b3_b = b0_b
        self_col = sb("self_col", [P, HEADS])
        a_cols = sb("a_cols", [P, 2])
        al = sb("al", [P, 2])
        half_neg = sb("half_neg", [P, NB])
        row_part = sb("row_part", [P, NB, NCH])
        col_part = sb("col_part", [P, NB, NS])
        rows = sb("rows", [P, NB])
        cols = sb("cols", [P, NB])
        inv_rows = sb("inv_rows", [P, NB])
        inv_cols = sb("inv_cols", [P, NB])
        d_nat = sb("d_nat", [P, NB])
        guard = sb("guard", [P, NB])
        inv0 = sb("inv0", [P, 4, 2])
        stage_a = sb("stage_a", [P, QW])
        stage_b = sb("stage_b", [P, QW])
        u_t = sb("u_t", [P, Q, D])
        v_t = sb("v_t", [P, Q, D])
        x1_st = [sb(f"x1_st{k}", [P, 2, 2, D], f16) for k in range(2)]
        stats = sb("stats", [P, Q, 6])
        mv = sb("mv", [P, Q, 2])
        var_e = sb("var_e", [P, Q])
        rstd = sb("rstd", [P, Q])
        s_nat = sb("s_nat", [P, NB, HEADS])
        row_max = sb("row_max", [P, HEADS, KV])
        neg_max = sb("neg_max", [P, 2, HEADS])
        row_sum = sb("row_sum", [P, NB, HEADS])
        inv_sum = sb("inv_sum", [P, HEADS])
        moment = sb("moment", [P, 1])

        ps = ctx.enter_context(nc.psum_tensor("ps", [P, 8 * 512], f32))
        bank = [ps[:, k * 512:(k + 1) * 512] for k in range(8)]
        tp_f = bank[0:4]
        ax_f = bank[4]
        atx_f = bank[5:7]
        ep_f = bank[7]
        acc = bank[0:2]
        ep = bank[2:6]
        leak_ps = [ps[:, k * 1024:k * 1024 + VW] for k in range(2)]
        tp_j = bank[4:6]
        av_j = bank[6]
        o_j = bank[7]

        def sem(name):
            return ctx.enter_context(nc.semaphore(name))

        s_const = sem("const_loaded")
        s_ident = sem("ident_ready")
        s_pool = sem("pool_setup")
        s_w0t = sem("w0t_transposed")
        s_set = sem("dve_setup")
        s_x0 = sem("x0_split")
        a_loaded = [sem(f"a_loaded{c}") for c in range(NCH)]
        at_stored = [sem(f"at_stored{c}") for c in range(NCH)]
        t_done, hi_done, lo_done = sem("a_transposed"), sem("at_hi"), sem("at_lo")
        sp_hi, sp_lo = sem("split_hi"), sem("split_lo")
        ax_done, qt_done = sem("ax_done"), sem("ax_taken")
        x0s_done, x0t_done, x0e_done = sem("x0_scaled"), sem("x0_transposed"), sem("x0t_taken")
        e1_done, var_f, rstd_f, x1_done, op1_done = (
            sem(n) for n in ("e1_done", "var_f", "rstd_f", "x1_done", "op1_done"))
        atx_done, atx_added = sem("atx_done"), sem("atx_added")
        ADDED_0 = K3
        link_f = sem("link_f")
        s_fin = sem("degrees_link")
        s_dpow = sem("degrees_pow")
        s_deg = sem("degrees_done")
        at_loaded = [sem(f"at_loaded{c}") for c in range(NCH)]
        at_used = sem("at_used")
        acc_done, acc_taken = sem("acc_done"), sem("acc_taken")
        ea_done = sem("ea_done")
        side_taken = sem("side_taken")
        var_q, rstd_q, mid_done = sem("var_q"), sem("rstd_q"), sem("mid_done")
        eb_done, eb_taken = sem("eb_done"), sem("eb_taken")
        ec_done, ops_done = sem("ec_done"), sem("ops_done")
        x_kept = sem("x_kept")
        link_q = sem("link_q")
        feat_t_taken, feat_done, ed_done, t_taken = (
            sem(n) for n in ("feat_t_taken", "feat_done", "ed_done", "t_taken"))
        s_late, s_neigh = sem("late_loaded"), sem("neigh_ready")
        m_loaded = [sem(f"m_loaded{k}") for k in range(2)]
        masked, bias_pool, fused = sem("masked"), sem("biased_by_pool"), sem("fused")
        t_whole_ready = sem("t_whole_ready")
        leaked, scored = sem("leaked"), sem("scored")
        max_done, exp_done = sem("max_done"), sem("exp_done")
        tp_done = [sem(f"tp_done{h}") for h in range(HEADS)]
        tp_act, tp_dve = sem("tp_by_act"), sem("tp_by_dve")
        av_done, o_taken, o_done = sem("av_done"), sem("o_taken"), sem("o_done")
        var_j, rstd_j, y_done, y_out = sem("var_j"), sem("rstd_j"), sem("y_done"), [sem(f"y_out{k}") for k in range(2)]
        link_j = sem("link_j")

        EARLY, LATE = 4 + 2 * HEADS, 6 + 2 * HEADS

        class Count:

            def __init__(self, engine, name, first):
                self.engine, self.reg = engine, engine.alloc_register(name)
                engine.reg_mov(self.reg, first)

            def wait(self, sem, step):
                self.engine.wait_ge(sem, self.reg)
                self.engine.reg_add(self.reg, self.reg, step)

        def scored_at(b, n):
            return PIECES * (b - (n < 0)) + LEAKED[n % len(LEAKED)] + 1

        def biased_at(par, n):
            return biased[(par * len(LEAKED) + n) % 4]

        block = ctx.enter_context(nc.Block())

        @block.sync
        def _(sp):
            def load_a(s, c):
                sp.dma_start(a_in[:, c], adj[ds(s * W, W), c * CW:(c + 1) * CW]
                             .rearrange("(r p) m -> p r m", p=P)).then_inc(a_loaded[c], 16)

            early = [(x_nat, x_in.rearrange("(b p) d -> p b d", p=P)), (w0_sb, w0),
                     (al[:, 0:1], alpha.partition_broadcast(P)), (b0_b[:], b0.partition_broadcast(P))]
            for h in range(HEADS):
                early.append((a_cols[h * C:(h + 1) * C, 0:1], a_self[h].unsqueeze(1)))
                early.append((a_cols[h * C:(h + 1) * C, 1:2], a_neigh[h].unsqueeze(1)))
            assert len(early) == EARLY
            load_a(0, 0)
            for to, of in early:
                sp.dma_start(to, of).then_inc(s_const, 16)
            for c in range(1, NCH):
                load_a(0, c)

            def super_f(s, last=False):
                for c in range(NCH):
                    sp.wait_ge(lo_done, s * J + (c + 1) * SPC)
                    sp.dma_start(at_dram[ds(s, 1), c].rearrange("o p x -> (o p) x"),
                                 at_out[:, c].rearrange("p m l w -> p (m l w)")).then_inc(at_stored[c], 16)
                    if not last:
                        sp.wait_ge(sp_lo, s * NCH + c + 1)
                        load_a(s + 1, c)

            super_f(0)
            with sp.Fori(1, NS - 1) as s:
                super_f(s)
            super_f(NS - 1, last=True)

            def load_at(q, c):
                sp.dma_start(at_in[:, c].rearrange("p s m l w -> p s (m l w)"),
                             at_dram[ds(2 * q, 2), c].rearrange("s p x -> p s x")).then_inc(at_loaded[c], 16)

            sp.wait_ge(atx_done, U3 * (NS - 1))
            for c in range(2):
                sp.wait_ge(at_stored[c], 16 * NS)
                load_at(0, c)
            sp.wait_ge(ax_done, J * NS)
            for c in range(NCH):
                sp.wait_ge(at_stored[c], 16 * NS)
            for c in range(2, NCH):
                load_at(0, c)
            sp.wait_ge(atx_done, U3 * NS)
            late = [(win_sb, w_in), (wout_sb, w_out), (w1_sb, w1), (w2_sb, w2),
                    (b1_b, b1.partition_broadcast(P)), (b2_b, b2.partition_broadcast(P))]
            for h in range(HEADS):
                late.append((w3_sb[:, h * C:(h + 1) * C], w3[h]))
                late.append((b3_b[:, h * C:(h + 1) * C], b3[h].partition_broadcast(P)))
            assert len(late) == LATE
            for to, of in late:
                sp.dma_start(to, of).then_inc(s_late, 16)

            for ph in range(3):
                with sp.Fori(1 if ph == 0 else 0, NQ) as q:
                    for c in range(NCH):
                        sp.wait_ge(at_used, (ph * NQ + q - 1) * NCH + c + 1)
                        load_at(q, c)

            def load_mask(b, k):
                sp.dma_start(mask[k], adj[ds(b * P, P), :]).then_inc(m_loaded[k], 16)

            def rows_out(b, k):
                sp.wait_ge(y_done, b + 1)
                sp.dma_start(out[ds(b * P, P), :], v_t[:, k, :]).then_inc(y_out[k], 16)

            sp.wait_ge(at_used, 2 * NQ * NCH)
            load_mask(0, 0)
            sp.wait_ge(at_used, 3 * NQ * NCH)
            load_mask(1, 1)
            for b in range(2):
                sp.wait_ge(scored, (b + 1) * HEADS * KV)
                load_mask(b + 2, b)
            with sp.Fori(1, NB // 2 - 1) as it:
                for k in range(2):
                    b = 2 * it + k
                    sp.wait_ge(scored, (b + 1) * HEADS * KV)
                    load_mask(b + 2, k)
                    rows_out(b - 2, k)
            for b in range(NB - 4, NB):
                rows_out(b, b % 2)
            for k in range(2):
                sp.wait_ge(y_out[k], 16 * (NB // 2))

        @block.gpsimd
        def _(pool):
            nc.gpsimd.memset(ident[:], 0.0).then_inc(s_pool, 1)
            nc.gpsimd.memset(half_neg[:], -0.5).then_inc(s_pool, 1)
            pool.wait_ge(s_pool, 2)
            nc.gpsimd.affine_select(out=ident[:], in_=ident[:], compare_op=ALU.not_equal, fill=1.0, base=0,
                                    pattern=[[-1, P]], channel_multiplier=1).then_inc(s_ident, 1)

            def rsqrt_f(s):
                pool.wait_ge(var_f, s + 1)
                nc.gpsimd.tensor_tensor(rstd[:, 0:2], var_e[:, 0:2], half_neg[:, 0:2], ALU.pow).then_inc(rstd_f, 1)

            def super_f(s, par, first=False):
                for c in range(NCH):
                    pool.wait_ge(sp_hi, (s * NCH + c + 1) * 2)
                    cc = slice(c * CW, (c + 1) * CW)
                    nc.gpsimd.tensor_tensor(split[par][:, :, 1, cc], a_in[:, c], split[par][:, :, 0, cc],
                                            ALU.subtract).then_inc(sp_lo, 1)
                    if c == 0 and not first:
                        rsqrt_f(s - 1)

            super_f(0, 0, first=True)
            super_f(1, 1)
            with pool.Fori(1, NS // 2) as it:
                for k in range(2):
                    super_f(2 * it + k, k)
            rsqrt_f(NS - 1)
            pool.wait_ge(s_fin, 5)
            nc.gpsimd.tensor_tensor(d_nat[:], cols[:], half_neg[:], ALU.pow).then_inc(s_dpow, 1)

            for ph, lots in ((0, NQ), (2, NQ)):
                with pool.Fori(0, lots) as q:
                    pool.wait_ge(var_q, (NQ if ph else 0) + q + 1)
                    nc.gpsimd.tensor_tensor(rstd[:], var_e[:], half_neg[:, 0:Q], ALU.pow).then_inc(rstd_q, 1)

            def bias_piece(b, par, i):
                h, k = divmod(i, KV)
                vs = slice(k * VW, (k + 1) * VW)
                piece = mask[par][:, vs]
                if h == 0:
                    nc.gpsimd.tensor_scalar(piece, piece, -1.0, NEG_MASK, ALU.add, ALU.mult).then_inc(masked, 1)
                if i in FUSED:
                    return
                n = LEAKED.index(i)
                pool.wait_ge(masked, b * KV + (k + 1 if h == 0 else KV))
                if not (isinstance(b, int) and b == 0 and n < 4):
                    pool.wait_ge(scored, scored_at(b, n - 4))
                nc.gpsimd.tensor_tensor(biased_at(par, n), piece, t_bcast[:, h, vs], ALU.add).then_inc(bias_pool, 1)

            def block_j(b, par, rsqrt_of=None):
                loads[par].wait(m_loaded[par], 16)
                for i in range(PIECES):
                    bias_piece(b, par, i)
                    if i == 5 and rsqrt_of is not None:
                        rsqrt_j(rsqrt_of)

            def rsqrt_j(b):
                pool.wait_ge(var_j, b + 1)
                nc.gpsimd.tensor_tensor(rstd[:, 0:1], var_e[:, 0:1], half_neg[:, 0:1], ALU.pow).then_inc(rstd_j, 1)

            loads = [Count(nc.gpsimd, f"mask_loads{k}", 16) for k in range(2)]
            pool.wait_ge(t_taken, NQ)
            for b in range(2):
                block_j(b, b)
            with pool.Fori(1, NB // 2) as it:
                for k in range(2):
                    block_j(2 * it + k, k, rsqrt_of=2 * it + k - 2)
            rsqrt_j(NB - 2)
            rsqrt_j(NB - 1)

        @block.scalar
        def _(act):
            act.wait_ge(s_set, 1)

            def hi_parts(s, j):
                c, jj = divmod(j, SPC)
                act.wait_ge(t_done, s * J + j + 1)
                if jj == 0 and not (isinstance(s, int) and s == 0):
                    act.wait_ge(at_stored[c], 16 * s)
                    act.wait_ge(ax_done, (s - 1) * J + (c + 1) * SPC)
                for k in range(2):
                    op = nc.scalar.activation(at_out[:, c, 2 * jj + k, 0, :], tp_f[j % 4][:, k * W:(k + 1) * W],
                                              ACT.Copy, accum_out=col_part[:, 2 * j + k, ds(s, 1)])
                op.then_inc(hi_done, 1)

            def split_hi(s, par, c, r):
                act.wait_ge(a_loaded[c], 16 * (s + 1))
                nc.scalar.activation(split[par][:, r, 0, c * CW:(c + 1) * CW], a_in[:, c, r, :], ACT.Copy,
                                     accum_out=row_part[:, ds(2 * s + r, 1), c]).then_inc(sp_hi, 1)

            def super_f(s, par, first=False):
                for j in range(J):
                    hi_parts(s, j)
                    if j in SPLIT:
                        c, r = SPLIT[j]
                        if r == 0 and not (isinstance(s, int) and s < 2):
                            act.wait_ge(atx_done, U3 * (s - 2) + (c + 1) * U3 // NCH)
                        split_hi(s, par, c, r)
                    if j == J_P3 and not first:
                        keep_x1(s - 1, 1 - par)
                    if j == J_X0:
                        if not first:
                            act.wait_ge(qt_done, s)
                        nc.scalar.activation(u_x0, x_nat[:, ds(2 * s, 2), :], ACT.Copy,
                                             scale=al[:, 1:2]).then_inc(x0s_done, 1)
                    if j == J_X0 + 1:
                        act.wait_ge(x0t_done, s + 1)
                        nc.scalar.activation(stage_b[:, 0:W], ep_f[:, 0:W], ACT.Copy).then_inc(x0e_done, 1)

            def keep_x1(s, par):
                act.wait_ge(x1_done, s + 1)
                nc.scalar.activation(op_odd[:, ds(2 * s, 2)], x1_st[par][:], ACT.Copy).then_inc(op1_done, 1)

            u_x0 = v_t[:, 2:4, :]
            super_f(0, 0, first=True)
            super_f(1, 1)
            with act.Fori(1, NS // 2) as it:
                for k in range(2):
                    super_f(2 * it + k, k)
            keep_x1(NS - 1, 1)

            def take_acc(t, half):
                act.wait_ge(at_used, (t + 1) * NCH)
                nc.scalar.activation(stage_a[:], acc[half][:], ACT.Copy).then_inc(acc_taken, 1)

            def take_eb(t):
                act.wait_ge(eb_done, t + 1)
                nc.scalar.activation(stage_b[:], ep[1][:], ACT.Copy).then_inc(eb_taken, 1)

            act.wait_ge(atx_added, ADDED_0 + NS * K3)
            with act.Fori(0, NQ // 2) as it:
                for k in range(2):
                    q = 2 * it + k
                    take_acc(q, k)
                    nc.scalar.activation(stage_b[:], at_x1[:, ds(q * QW, QW)], ACT.Copy).then_inc(side_taken, 1)
                    take_eb(q)
            with act.Fori(0, NQ // 2) as it:
                for k in range(2):
                    t = NQ + 2 * it + k
                    take_acc(t, k)
                    take_eb(t)
            with act.Fori(0, NQ // 2) as it:
                for k in range(2):
                    q = 2 * it + k
                    take_acc(2 * NQ + q, k)
                    take_eb(2 * NQ + q)
                    act.wait_ge(ec_done, 2 * NQ + q + 1)
                    nc.scalar.activation(stage_a[:], ep[2][:], ACT.Copy).then_inc(feat_t_taken, 1)
                    act.wait_ge(ed_done, q + 1)
                    for h in range(HEADS):
                        nc.scalar.activation(t_bcast[:, h, ds(q * QW, QW)], ep[h][:], ACT.Copy, scale=LEAK)
                    nc.scalar.activation(s_nat[:, ds(q * Q, Q), :],
                                         ep[3][:, 0:Q * HEADS].rearrange("p (r h) -> p r h", h=HEADS),
                                         ACT.Copy, scale=1.0 - LEAK).then_inc(t_taken, 1)

            def leak(b, i):
                h, k = divmod(i, KV)
                n = LEAKED.index(i)
                if not (isinstance(b, int) and b == 0 and n < 2):
                    to = (0, n + 1) if n + 1 < len(LEAKED) else (1, 0)
                    pieces_scored.wait(scored, scored_at(to[0], to[1] - 2) - scored_at(0, n - 2))
                nc.scalar.activation(leak_ps[n % 2], t_bcast[:, h, k * VW:(k + 1) * VW], ACT.Relu,
                                     bias=s_nat[:, ds(b, 1), h], scale=(1.0 - LEAK) / LEAK).then_inc(leaked, 1)

            def expo(b, par, h):
                act.wait_ge(max_done, b * HEADS + h + 1)
                nc.scalar.activation(prob[par][h], prob[par][h], ACT.Exp, bias=neg_max[:, par, h:h + 1],
                                     accum_out=row_sum[:, ds(b, 1), h]).then_inc(exp_done, 1)

            def take_tp(b, g, h):
                act.wait_ge(tp_done[h], b * G4 + g + 1)
                if not (isinstance(b, int) and b == 0 and g < 2):
                    act.wait_ge(av_done, b * G4 + g - 1)
                nc.scalar.activation(pt[g % 2][h], tp_j[h], ACT.Copy).then_inc(tp_act, 1)

            def take_out(b):
                act.wait_ge(av_done, (b + 1) * G4)
                if not (isinstance(b, int) and b == 0):
                    act.wait_ge(o_done, b)
                nc.scalar.activation(stage_a[:, 0:P], av_j[:, 0:P], ACT.Copy).then_inc(o_taken, 1)

            def block_j(b, par, first=False, last=False):
                for step in ACT_PLAN.split():
                    what, i = step[0], int(step[1])
                    if what == "L" and not last:
                        leak(b + 1, i)
                    if what == "X" and not last:
                        expo(b + 1, 1 - par, i)
                    if what == "T":
                        take_tp(b, i, int(step[2]))
                    if what == "O" and not first:
                        take_out(b - 1)

            pieces_scored = Count(nc.scalar, "pieces_scored", scored_at(0, 0))
            act.wait_ge(t_taken, NQ)
            for i in LEAKED:
                leak(0, i)
            for h in range(HEADS):
                expo(0, 0, h)
            block_j(0, 0, first=True)
            block_j(1, 1)
            with act.Fori(1, NB // 2 - 1) as it:
                for k in range(2):
                    block_j(2 * it + k, k)
            block_j(NB - 2, 0)
            block_j(NB - 1, 1, last=True)
            take_out(NB - 1)

        @block.vector
        def _(dve):
            dve.wait_ge(s_const, 16 * EARLY)
            nc.vector.tensor_scalar(al[:, 1:2], al[:, 0:1], -1.0, 1.0, ALU.mult, ALU.add).then_inc(s_set, 1)
            nc.vector.tensor_copy(op_even[:, :, 0, :], x_nat).then_inc(s_set, 1)
            nc.vector.memset(self_col[:], 0.0).then_inc(atx_added, ADDED_0)
            nc.vector.memset(at_x1, 0.0).then_inc(s_set, 1)
            dve.wait_ge(s_set, 3)
            nc.vector.tensor_tensor(op_even[:, :, 1, :], x_nat, op_even[:, :, 0, :], ALU.subtract).then_inc(s_x0, 1)
            for h in range(HEADS):
                hc = slice(h * C, (h + 1) * C)
                nc.vector.tensor_copy(self_col[hc, h:h + 1], a_cols[hc, 0:1])
            dve.wait_ge(s_w0t, 1)
            nc.vector.tensor_copy(w0t[:], ep_f[:, 0:P]).then_inc(s_set, 1)

            def lo_parts(s, j):
                c, jj = divmod(j, SPC)
                dve.wait_ge(hi_done, s * J + j + 1)
                nc.vector.tensor_tensor(at_out[:, c, 2 * jj:2 * jj + 2, 1, :],
                                        tp_f[j % 4][:].rearrange("p (m w) -> p m w", m=2),
                                        at_out[:, c, 2 * jj:2 * jj + 2, 0, :], ALU.subtract).then_inc(lo_done, 1)

            def chain(base, counter):
                at = [base]

                def link(op):
                    at[0] = at[0] + 1
                    op.then_inc(counter, 1)
                    dve.wait_ge(counter, at[0])
                return link

            LINKS = 14

            def take_ax(s):
                dve.wait_ge(ax_done, (s + 1) * J)
                dve.wait_ge(x0e_done, s + 1)
                nc.vector.scalar_tensor_tensor(out=stage_a[:, 0:W], in0=ax_f[:, 0:W], scalar=al[:, 0:1],
                                               in1=stage_b[:, 0:W], op0=ALU.mult, op1=ALU.add).then_inc(qt_done, 1)

            def degree(s, part):
                link = chain(s * LINKS + 4 * part, link_f)
                if part == 0:
                    dve.wait_ge(sp_hi, (s + 1) * NCH * 2)
                    link(nc.vector.tensor_reduce(rows[:, ds(2 * s, 2)], row_part[:, ds(2 * s, 2), :], AX.X, ALU.add))
                    link(nc.vector.tensor_scalar(inv0[:, 0, :], rows[:, ds(2 * s, 2)], al[:, 0:1], al[:, 1:2],
                                                 ALU.mult, ALU.add))
                    link(nc.vector.tensor_scalar(inv0[:, 1, :], inv0[:, 0, :], 0.0, None, ALU.is_equal))
                    link(nc.vector.tensor_tensor(inv0[:, 2, :], inv0[:, 0, :], inv0[:, 1, :], ALU.add))
                else:
                    link(nc.vector.reciprocal(inv0[:, 3, :], inv0[:, 2, :]))
                    link(nc.vector.tensor_tensor(inv0[:, 0, :], inv0[:, 3, :], inv0[:, 1, :], ALU.mult))
                    link(nc.vector.tensor_tensor(inv0[:, 3, :], inv0[:, 3, :], inv0[:, 0, :], ALU.subtract))

            def stats_f(s, part):
                link = chain(s * LINKS + (7, 8, 10)[part], link_f)
                if part == 0:
                    dve.wait_ge(e1_done, s + 1)
                    for r in range(2):
                        op = nc.vector.scalar_tensor_tensor(out=u_t[:, r, :], in0=ep_f[:, r * P:(r + 1) * P],
                                                            scalar=inv0[:, 3, r:r + 1], in1=b0_b[:],
                                                            op0=ALU.mult, op1=ALU.add)
                    link(op)
                if part == 1:
                    link(nc.vector.scalar_tensor_tensor(out=u_t[:, 0:2, :], in0=u_t[:, 0:2, :], scalar=0.0,
                                                        in1=x_nat[:, ds(2 * s, 2), :], op0=ALU.max, op1=ALU.add))
                    for r in range(2):
                        op = nc.vector.bn_stats(stats[:, r, :], u_t[:, r, :])
                    link(op)
                    nc.vector.memset(moment[:], 0.0)
                if part == 2:
                    for r in range(2):
                        op = nc.vector.bn_aggr(mv[:, r, :], stats[:, r, :])
                    link(op)
                    nc.vector.tensor_scalar(var_e[:, 0:2], mv[:, 0:2, 1], EPS, None, ALU.add).then_inc(var_f, 1)

            def norm_f(s, par, part):
                link = chain(s * LINKS + 11 + 2 * part, link_f)
                if part == 0:
                    dve.wait_ge(rstd_f, s + 1)
                    for r in range(2):
                        op = nc.vector.tensor_scalar(v_t[:, r, :], u_t[:, r, :], mv[:, r, 0:1], rstd[:, r:r + 1],
                                                     ALU.subtract, ALU.mult)
                    link(op)
                    dve.wait_ge(x0s_done, s + 1)
                    link(nc.vector.tensor_scalar(x_nat[:, ds(2 * s, 2), :], v_t[:, 0:2, :], 1.0, None, ALU.mult))
                else:
                    if not (isinstance(s, int) and s < 2):
                        dve.wait_ge(atx_done, U3 * (s - 1))
                        dve.wait_ge(op1_done, s - 1)
                    link(nc.vector.tensor_copy(x1_st[par][:, :, 0, :], v_t[:, 0:2, :]))
                    nc.vector.tensor_tensor(x1_st[par][:, :, 1, :], v_t[:, 0:2, :], x1_st[par][:, :, 0, :],
                                            ALU.subtract).then_inc(x1_done, 1)

            def add_atx(s, k):
                n = s * K3 + k
                dve.wait_ge(atx_done, s * U3 + 2 * k + 2)
                if not (isinstance(s, int) and s == 0):
                    dve.wait_ge(atx_added, ADDED_0 + n - K3 + 1)
                piece = at_x1[:, k * 512:(k + 1) * 512]
                nc.vector.tensor_tensor(piece, atx_f[k % 2][:], piece, ALU.add).then_inc(atx_added, 1)

            EPILOGUE = {J_TAKE: take_ax, J_DEG: lambda s: degree(s, 0), J_DEG + 1: lambda s: degree(s, 1)}
            EPILOGUE |= {J_RELU + k: (lambda s, k=k: stats_f(s, k)) for k in range(3)}

            def super_f(s, par):
                for j in range(J):
                    lo_parts(s, j)
                    if not (isinstance(s, int) and s == 0):
                        if j in EPILOGUE:
                            EPILOGUE[j](s - 1)
                        if j in (J_NORM, J_NORM + 1):
                            norm_f(s - 1, 1 - par, j - J_NORM)
                    of, u = unit_at(s, j)
                    if u % 2 and not (isinstance(of, int) and of < 0):
                        add_atx(of, u // 2)

            super_f(0, 0)
            super_f(1, 1)
            with dve.Fori(1, NS // 2) as it:
                for k in range(2):
                    super_f(2 * it + k, k)
            for j in sorted(EPILOGUE):
                EPILOGUE[j](NS - 1)
            norm_f(NS - 1, 1, 0)
            norm_f(NS - 1, 1, 1)
            for j in range(J_P3):
                of, u = unit_at(NS, j)
                if u % 2:
                    add_atx(of, u // 2)
            for k in range(K3):
                add_atx(NS - 1, k)

            n_fin = [0]

            def link(op):
                n_fin[0] += 1
                op.then_inc(s_fin, 1)
                dve.wait_ge(s_fin, n_fin[0])

            def where_positive(to, of):
                link(nc.vector.tensor_scalar(guard[:], of, 0.0, None, ALU.is_gt))
                link(nc.vector.tensor_tensor(to, of, guard[:], ALU.mult))
                link(nc.vector.tensor_scalar(inv_cols[:], guard[:], -1.0, 1.0, ALU.mult, ALU.add))
                link(nc.vector.tensor_tensor(to, to, inv_cols[:], ALU.add))

            link(nc.vector.tensor_scalar(inv_rows[:], rows[:], 1.0, None, ALU.add))
            where_positive(cols[:], inv_rows[:])
            assert n_fin[0] == 5
            dve.wait_ge(s_dpow, 1)
            link(nc.vector.tensor_tensor(d_nat[:], d_nat[:], guard[:], ALU.mult))
            dve.wait_ge(hi_done, NS * J)
            link(nc.vector.tensor_reduce(cols[:], col_part[:], AX.X, ALU.add))
            where_positive(inv_rows[:], rows[:])
            link(nc.vector.reciprocal(inv_rows[:], inv_rows[:]))
            where_positive(rows[:], cols[:])
            link(nc.vector.reciprocal(inv_cols[:], rows[:]))
            dve.wait_ge(s_late, 16 * LATE)
            link(nc.vector.memset(neigh_b, 0.0))
            for h in range(HEADS):
                hc = slice(h * C, (h + 1) * C)
                op = nc.vector.tensor_copy(neigh_b[hc, h, :], a_cols[hc, 1:2].to_broadcast([C, P]))
            op.then_inc(s_neigh, 1)

            LG, LH, LI = 8, 5, 6

            def layernorm_in(link):
                for r in range(Q):
                    op = nc.vector.bn_stats(stats[:, r, :], u_t[:, r, :])
                link(op)
                nc.vector.memset(moment[:], 0.0)
                for r in range(Q):
                    op = nc.vector.bn_aggr(mv[:, r, :], stats[:, r, :])
                link(op)
                nc.vector.tensor_scalar(var_e[:], mv[:, :, 1], EPS, None, ALU.add).then_inc(var_q, 1)

            def layernorm_out(link, q, n, t):
                dve.wait_ge(rstd_q, n)
                for r in range(Q):
                    op = nc.vector.tensor_scalar(v_t[:, r, :], u_t[:, r, :], mv[:, r, 0:1], rstd[:, r:r + 1],
                                                 ALU.subtract, ALU.mult)
                op.then_inc(mid_done, 1)
                dve.wait_ge(mid_done, t + 1)
                link(nc.vector.tensor_scalar(x_nat[:, ds(Q * q, Q), :], v_t[:], 1.0, None, ALU.mult))

            def operands(link, q, t, to):
                dve.wait_ge(ec_done, t + 1)
                for r in range(Q):
                    op = nc.vector.tensor_scalar(u_t[:, r, :], ep[2][:, r * P:(r + 1) * P],
                                                 d_nat[:, ds(Q * q + r, 1)], None, ALU.mult)
                link(op)
                link(nc.vector.tensor_scalar(y_nat[:, ds(Q * q, Q), :], u_t[:], 1.0, None, ALU.mult))
                link(nc.vector.tensor_scalar(to[:, ds(Q * q, Q), 0, :], u_t[:], 1.0, None, ALU.mult))
                nc.vector.tensor_tensor(to[:, ds(Q * q, Q), 1, :], u_t[:], to[:, ds(Q * q, Q), 0, :],
                                        ALU.subtract).then_inc(ops_done, 1)
                dve.wait_ge(ops_done, t + 1)

            with dve.Fori(0, NQ) as q:
                link = chain(q * LG, link_q)
                dve.wait_ge(ea_done, q + 1)
                for r in range(Q):
                    op = nc.vector.scalar_tensor_tensor(out=u_t[:, r, :], in0=ep[0][:, r * P:(r + 1) * P],
                                                        scalar=inv_rows[:, ds(Q * q + r, 1)],
                                                        in1=x_nat[:, ds(Q * q + r, 1), :].rearrange("p o d -> p (o d)"),
                                                        op0=ALU.mult, op1=ALU.add)
                link(op)
                for r in range(Q):
                    op = nc.vector.scalar_tensor_tensor(out=u_t[:, r, :], in0=ep[3][:, r * P:(r + 1) * P],
                                                        scalar=inv_cols[:, ds(Q * q + r, 1)], in1=u_t[:, r, :],
                                                        op0=ALU.mult, op1=ALU.add)
                link(op)
                layernorm_in(link)
                layernorm_out(link, q, q + 1, q)
                operands(link, q, q, op_even)

            with dve.Fori(0, NQ) as q:
                link = chain(NQ * LG + q * LH, link_q)
                dve.wait_ge(ea_done, NQ + q + 1)
                yq = y_nat[:, ds(Q * q, Q), :]
                link(nc.vector.tensor_tensor(u_t[:], ep[0][:].rearrange("p (r d) -> p r d", r=Q), yq, ALU.add))
                for r in range(Q):
                    op = nc.vector.scalar_tensor_tensor(out=v_t[:, r, :], in0=u_t[:, r, :],
                                                        scalar=d_nat[:, ds(Q * q + r, 1)], in1=b1_b[:],
                                                        op0=ALU.mult, op1=ALU.add)
                link(op)
                nc.vector.tensor_scalar(v_t[:], v_t[:], 0.0, None, ALU.max).then_inc(mid_done, 1)
                operands(link, q, NQ + q, op_odd)

            with dve.Fori(0, NQ) as q:
                link = chain(NQ * (LG + LH) + q * LI, link_q)
                t = 2 * NQ + q
                dve.wait_ge(ea_done, t + 1)
                yq = y_nat[:, ds(Q * q, Q), :]
                link(nc.vector.tensor_tensor(u_t[:], ep[0][:].rearrange("p (r d) -> p r d", r=Q), yq, ALU.add))
                for r in range(Q):
                    op = nc.vector.scalar_tensor_tensor(out=u_t[:, r, :], in0=u_t[:, r, :],
                                                        scalar=d_nat[:, ds(Q * q + r, 1)], in1=b2_b[:],
                                                        op0=ALU.mult, op1=ALU.add)
                link(op)
                link(nc.vector.tensor_tensor(u_t[:], u_t[:], x_nat[:, ds(Q * q, Q), :], ALU.add))
                layernorm_in(link)
                layernorm_out(link, q, NQ + q + 1, t)
                dve.wait_ge(feat_done, q + 1)
                nc.vector.tensor_scalar(feats[:, ds(Q * q, Q), :], ep[3][:].rearrange("p (r d) -> p r d", r=Q), 1.0, None,
                                        ALU.mult).then_inc(ops_done, 1)

            def free_probs(b, h):
                if not (isinstance(b, int) and b < 2):
                    dve.wait_ge(tp_done[h], (b - 1) * G4)

            def fuse(b, par, i):
                h, k = divmod(i, KV)
                vs = slice(k * VW, (k + 1) * VW)
                free_probs(b, h)
                nc.vector.scalar_tensor_tensor(out=prob[par][h][:, vs], in0=t_whole[FUSED.index(i)],
                                               scalar=s_nat[:, ds(b, 1), h], in1=t_bcast[:, h, vs],
                                               op0=ALU.add, op1=ALU.max).then_inc(fused, 1)

            def score(b, par, i):
                h, k = divmod(i, KV)
                vs = slice(k * VW, (k + 1) * VW)
                if i in FUSED:
                    dve.wait_ge(masked, b * KV + (k + 1 if h == 0 else KV))
                    pieces_fused.wait(fused, 1)
                    leaky, bias = prob[par][h][:, vs], mask[par][:, vs]
                else:
                    n = LEAKED.index(i)
                    free_probs(b, h)
                    dve.wait_ge(bias_pool, b * len(LEAKED) + n + 1)
                    pieces_leaked.wait(leaked, 1)
                    leaky, bias = leak_ps[n % 2], biased_at(par, n)
                nc.vector.tensor_tensor_reduce(out=prob[par][h][:, vs], in0=leaky, in1=bias,
                                               scale=1.0, scalar=LOWEST, op0=ALU.add, op1=ALU.max,
                                               accum_out=row_max[:, h, k:k + 1]).then_inc(scored, 1)

            def maximum(b, par, h):
                dve.wait_ge(scored, b * HEADS * KV + (h + 1) * KV)
                if not (isinstance(b, int) and b < 2):
                    dve.wait_ge(exp_done, (b - 1) * HEADS)
                nc.vector.tensor_reduce(neg_max[:, par, h:h + 1], row_max[:, h, :], AX.X, ALU.max,
                                        negate=True).then_inc(max_done, 1)

            def take_tp(b, g, h):
                dve.wait_ge(tp_done[h], b * G4 + g + 1)
                if not (isinstance(b, int) and b == 0 and g < 2):
                    dve.wait_ge(av_done, b * G4 + g - 1)
                nc.vector.tensor_copy(pt[g % 2][h], tp_j[h]).then_inc(tp_dve, 1)

            LJ = 5

            def stats_j(b, par):
                link = chain(b * LJ, link_j)
                dve.wait_ge(o_done, b + 1)
                link(nc.vector.reciprocal(inv_sum[:], row_sum[:, ds(b, 1), :].rearrange("p o h -> p (o h)")))
                for h in range(HEADS):
                    hc = slice(h * C, (h + 1) * C)
                    op = nc.vector.scalar_tensor_tensor(out=u_t[:, 0, hc], in0=o_j[:, hc], scalar=inv_sum[:, h:h + 1],
                                                        in1=b3_b[:, hc], op0=ALU.mult, op1=ALU.add)
                link(op)
                link(nc.vector.scalar_tensor_tensor(out=u_t[:, 0, :], in0=u_t[:, 0, :], scalar=0.0,
                                                    in1=x_nat[:, ds(b, 1), :].rearrange("p o d -> p (o d)"),
                                                    op0=ALU.max, op1=ALU.add))
                link(nc.vector.bn_stats(stats[:, 0, :], u_t[:, 0, :]))
                nc.vector.memset(moment[:], 0.0)
                link(nc.vector.bn_aggr(mv[:, 0, :], stats[:, 0, :]))
                nc.vector.tensor_scalar(var_e[:, 0:1], mv[:, 0, 1:2], EPS, None, ALU.add).then_inc(var_j, 1)

            def norm_j(b, n, par):
                dve.wait_ge(rstd_j, b + 1)
                if not (isinstance(n, int) and n == 0):
                    dve.wait_ge(y_out[par], 16 * n)
                nc.vector.tensor_scalar(v_t[:, par, :], u_t[:, 0, :], mv[:, 0, 0:1], rstd[:, 0:1],
                                        ALU.subtract, ALU.mult).then_inc(y_done, 1)

            def block_j(b, n, par, first=False, last=False):
                for step in DVE_PLAN.split():
                    what, i = step[0], int(step[1])
                    if what == "F" and not last:
                        fuse(b + 1, 1 - par, i)
                    if what == "S" and not last:
                        score(b + 1, 1 - par, i)
                        if i == KV:
                            maximum(b + 1, 1 - par, 0)
                    if what == "M" and not last:
                        maximum(b + 1, 1 - par, 1)
                    if what == "V":
                        take_tp(b, i, int(step[2]))
                    if what == "O" and not first:
                        stats_j(b - 1, 1 - par)
                    if what == "N" and not first:
                        norm_j(b - 1, n - (1 - par), 1 - par)

            pieces_leaked = Count(nc.vector, "pieces_leaked", 1)
            pieces_fused = Count(nc.vector, "pieces_fused", 1)
            dve.wait_ge(t_taken, NQ)
            for k, i in enumerate(FUSED):
                h, kk = divmod(i, KV)
                op = nc.vector.tensor_scalar(t_whole[k], t_bcast[:, h, kk * VW:(kk + 1) * VW], 1.0 / LEAK, None,
                                             ALU.mult)
            op.then_inc(t_whole_ready, 1)
            dve.wait_ge(t_whole_ready, 1)
            for i in range(HEADS * KV):
                if i in FUSED:
                    fuse(0, 0, i)
                score(0, 0, i)
                if i % KV == KV - 1:
                    maximum(0, 0, i // KV)
            block_j(0, 0, 0, first=True)
            block_j(1, 0, 1)
            with dve.Fori(1, NB // 2 - 1) as it:
                for k in range(2):
                    block_j(2 * it + k, it, k)
            block_j(NB - 2, NB // 2 - 1, 0)
            block_j(NB - 1, NB // 2 - 1, 1, last=True)
            stats_j(NB - 1, 1)
            norm_j(NB - 1, NB // 2 - 1, 1)

        @block.tensor
        def _(pe):
            pe.wait_ge(s_ident, 1)
            pe.wait_ge(s_const, 16 * EARLY)
            nc.tensor.transpose(ep_f[:, 0:P], w0_sb, ident[:]).then_inc(s_w0t, 1)

            def transposes(s, j):
                c, jj = divmod(j, SPC)
                if jj == 0:
                    pe.wait_ge(a_loaded[c], 16 * (s + 1))
                if not (isinstance(s, int) and s == 0 and j < 4):
                    pe.wait_ge(lo_done, s * J + j - 3)
                for k in range(2):
                    for r in range(2):
                        m = (2 * jj + k) * P
                        op = nc.tensor.transpose(tp_f[j % 4][:, k * W + r * P:k * W + (r + 1) * P],
                                                 a_in[:, c, r, m:m + P], ident[:])
                op.then_inc(t_done, 1)

            def ax_step(s, j):
                c, jj = divmod(j, SPC)
                pe.wait_ge(lo_done, s * J + j + 1)
                if j == 0 and not (isinstance(s, int) and s == 0):
                    pe.wait_ge(qt_done, s)
                for k in range(2):
                    m = 2 * j + k
                    hi, lo = (at_out[:, c, 2 * jj + k, z, :] for z in range(2))
                    nc.tensor.matmul(ax_f[:, 0:W], op_even[:, m, 0, :], hi, start=(m == 0), stop=False)
                    nc.tensor.matmul(ax_f[:, 0:W], op_even[:, m, 0, :], lo, start=False, stop=False)
                    op = nc.tensor.matmul(ax_f[:, 0:W], op_even[:, m, 1, :], hi, start=False, stop=(m == NB - 1))
                op.then_inc(ax_done, 1)

            def layer0(s):
                pe.wait_ge(qt_done, s + 1)
                for r in range(2):
                    op = nc.tensor.matmul(ep_f[:, r * P:(r + 1) * P], stage_a[:, r * P:(r + 1) * P], w0t[:],
                                          start=True, stop=True)
                op.then_inc(e1_done, 1)

            def x0_transposed(s):
                pe.wait_ge(x0s_done, s + 1)
                if not (isinstance(s, int) and s == 0):
                    pe.wait_ge(var_f, s)
                for r in range(2):
                    op = nc.tensor.transpose(ep_f[:, r * P:(r + 1) * P], v_t[:, 2 + r, :], ident[:])
                op.then_inc(x0t_done, 1)

            def atx_unit(s, par, u):
                k, r = divmod(u, 2)
                if u == 0:
                    pe.wait_ge(x1_done, s + 1)
                if r == 0:
                    pe.wait_ge(sp_lo, s * NCH + ((k + 1) * 512 - 1) // CW + 1)
                    if not (isinstance(s, int) and s == 0 and k < 2):
                        pe.wait_ge(atx_added, ADDED_0 + s * K3 + k - 1)
                hi, lo = (split[par][:, r, z, k * 512:(k + 1) * 512] for z in range(2))
                nc.tensor.matmul(atx_f[k % 2], x1_st[par][:, r, 0, :], hi, start=(r == 0), stop=False)
                nc.tensor.matmul(atx_f[k % 2], x1_st[par][:, r, 0, :], lo, start=False, stop=False)
                nc.tensor.matmul(atx_f[k % 2], x1_st[par][:, r, 1, :], hi, start=False, stop=(r == 1)).then_inc(atx_done, 1)

            def super_f(s, par):
                for j in range(J):
                    transposes(s, j)
                    of, u = unit_at(s, j)
                    if not (isinstance(of, int) and of < 0):
                        atx_unit(of, 1 - par if j >= J_P3 else par, u)
                    if j >= 2:
                        ax_step(s, j - 2)
                    elif not (isinstance(s, int) and s == 0):
                        ax_step(s - 1, J - 2 + j)
                    if j == J_E1 and not (isinstance(s, int) and s == 0):
                        layer0(s - 1)
                    if j == J_X0 + 1:
                        x0_transposed(s)

            pe.wait_ge(s_set, 4)
            pe.wait_ge(s_x0, 1)
            super_f(0, 0)
            super_f(1, 1)
            with pe.Fori(1, NS // 2) as it:
                for k in range(2):
                    super_f(2 * it + k, k)
            ax_step(NS - 1, J - 2)
            ax_step(NS - 1, J - 1)
            for j in range(J_P3):
                if j == J_E1:
                    layer0(NS - 1)
                of, u = unit_at(NS, j)
                atx_unit(of, 0, u)
            for u in range(U3):
                atx_unit(NS - 1, 1, u)

            def chunk(ph, q, half, c):
                t = ph * NQ + q
                y = (op_odd, op_even, op_odd)[ph]
                pe.wait_ge(at_loaded[c], 16 * (t + 1))
                if isinstance(q, int) and q == 0:
                    if ph == 0:
                        pe.wait_ge(op1_done, NS)
                    else:
                        pe.wait_ge(ops_done, (ph - 1) * NQ - (-(c + 1) * NQ // NCH))
                if c == 0 and not (isinstance(t, int) and t < 2):
                    pe.wait_ge(acc_taken, t - 1)
                for m in range(MC):
                    b = c * MC + m
                    hi, lo = (at_in[:, c, :, m, z, :] for z in range(2))
                    to = acc[half].rearrange("p (s w) -> p s w", s=2)
                    nc.tensor.matmul(to, y[:, b, 0, :], hi, start=(b == 0), stop=False)
                    nc.tensor.matmul(to, y[:, b, 0, :], lo, start=False, stop=False)
                    op = nc.tensor.matmul(to, y[:, b, 1, :], hi, start=False, stop=(b == NB - 1))
                op.then_inc(at_used, 1)

            def four(to, of, weights):
                for r in range(Q):
                    op = nc.tensor.matmul(to[:, r * P:(r + 1) * P], of[:, r * P:(r + 1) * P], weights,
                                          start=True, stop=True)
                return op

            def four_transposes(to, of):
                for r in range(Q):
                    op = nc.tensor.transpose(to[:, r * P:(r + 1) * P], of(r), ident[:])
                return op

            def epilogue_a(ph, q):
                t = ph * NQ + q
                pe.wait_ge(acc_taken, t + 1)
                if ph == 0:
                    pe.wait_ge(side_taken, q + 1)
                    four(ep[3], stage_b, wout_sb)
                    four(ep[0], stage_a, win_sb).then_inc(ea_done, 1)
                else:
                    if ph == 2 and not (isinstance(q, int) and q == 0):
                        pe.wait_ge(t_taken, q)
                    four_transposes(ep[0], lambda r: stage_a[:, r * P:(r + 1) * P]).then_inc(ea_done, 1)

            def epilogue_b(ph, q):
                pe.wait_ge(mid_done, ph * NQ + q + 1)
                four_transposes(ep[1], lambda r: v_t[:, r, :]).then_inc(eb_done, 1)

            def epilogue_c(ph, q):
                t = ph * NQ + q
                pe.wait_ge(eb_taken, t + 1)
                if not (isinstance(t, int) and t == 0):
                    pe.wait_ge(ops_done, t)
                if ph < 2:
                    four(ep[2], stage_b, (w1_sb, w2_sb)[ph]).then_inc(ec_done, 1)
                    return
                nc.tensor.matmul(ep[2], w3_sb, stage_b[:], start=True, stop=True).then_inc(ec_done, 1)
                four(ep[3], stage_b, w3_sb).then_inc(feat_done, 1)
                pe.wait_ge(feat_t_taken, q + 1)
                for h in range(HEADS):
                    nc.tensor.matmul(ep[h], neigh_b[:, h, :], stage_a[:], start=True, stop=True)
                pe.wait_ge(ops_done, t + 1)
                for r in range(Q):
                    op = nc.tensor.matmul(ep[3][:, r * HEADS:(r + 1) * HEADS], stage_a[:, r * P:(r + 1) * P],
                                          self_col[:], start=True, stop=True)
                op.then_inc(ed_done, 1)

            def quad(ph, q, half, before=None):
                chunk(ph, q, half, 0)
                if before:
                    epilogue_a(*before)
                chunk(ph, q, half, 1)
                if before:
                    epilogue_b(*before)
                chunk(ph, q, half, 2)
                if before:
                    epilogue_c(*before)
                chunk(ph, q, half, 3)

            quad(0, 0, 0)
            pe.wait_ge(s_late, 16 * LATE)
            pe.wait_ge(atx_added, ADDED_0 + NS * K3)
            quad(0, 1, 1, (0, 0))
            with pe.Fori(1, NQ // 2) as it:
                for k in range(2):
                    quad(0, 2 * it + k, k, (0, 2 * it + k - 1))
            for ph in (1, 2):
                if ph == 2:
                    pe.wait_ge(s_neigh, 1)
                quad(ph, 0, 0, (ph - 1, NQ - 1))
                quad(ph, 1, 1, (ph, 0))
                with pe.Fori(1, NQ // 2) as it:
                    for k in range(2):
                        quad(ph, 2 * it + k, k, (ph, 2 * it + k - 1))
            epilogue_a(2, NQ - 1)
            epilogue_b(2, NQ - 1)
            epilogue_c(2, NQ - 1)

            def taken(b, g, h):
                for by, counter in ((BY_ACT, tp_act), (BY_DVE, tp_dve)):
                    if (g, h) in by:
                        pe.wait_ge(counter, b * len(by) + by.index((g, h)) + 1)

            def tp_group(b, par, g):
                for h in range(HEADS):
                    if g == 0:
                        pe.wait_ge(exp_done, b * HEADS + h + 1)
                        if not (isinstance(b, int) and b == 0):
                            taken(b - 1, G4 - 1, h)
                    else:
                        taken(b, g - 1, h)
                    for k in range(4):
                        m = (4 * g + k) * P
                        op = nc.tensor.transpose(tp_j[h][:, k * P:(k + 1) * P], prob[par][h][:, m:m + P], ident[:])
                    op.then_inc(tp_done[h], 1)

            def av_group(b, g):
                for h in range(HEADS):
                    taken(b, g, h)
                if g == 0 and not (isinstance(b, int) and b == 0):
                    pe.wait_ge(o_taken, b)
                for k in range(4):
                    m = 4 * g + k
                    for h in range(HEADS):
                        hc = slice(h * C, (h + 1) * C)
                        op = nc.tensor.matmul(av_j[hc, 0:P], feats[:, m, hc], pt[g % 2][h][:, k * P:(k + 1) * P],
                                              start=(m == 0), stop=(m == NB - 1))
                op.then_inc(av_done, 1)

            def out_rows(b):
                pe.wait_ge(o_taken, b + 1)
                if not (isinstance(b, int) and b == 0):
                    pe.wait_ge(var_j, b)
                nc.tensor.transpose(o_j[:, 0:P], stage_a[:, 0:P], ident[:]).then_inc(o_done, 1)

            def block_j(b, par, first=False):
                for g in range(G4):
                    tp_group(b, par, g)
                    if g == 1 and not first:
                        out_rows(b - 1)
                    if g >= 1:
                        av_group(b, g - 1)
                av_group(b, G4 - 1)

            pe.wait_ge(ops_done, 3 * NQ)
            block_j(0, 0, first=True)
            block_j(1, 1)
            with pe.Fori(1, NB // 2) as it:
                for k in range(2):
                    block_j(2 * it + k, k)
            out_rows(NB - 1)


_INS = ["x", "adj", "L0_gnn_alpha", "L0_gnn_W", "L0_gnn_b", "L1_gnn_W_in", "L1_gnn_W_out", "L2_gnn_W1", "L2_gnn_b1",
        "L2_gnn_W2", "L2_gnn_b2", "L3_gnn_W", "L3_gnn_a_self", "L3_gnn_a_neigh", "L3_gnn_b"]


def kernel(**inputs):
    import numpy as _np
    import concourse.bacc as _bacc
    from concourse import mybir as _mybir
    from concourse.bass_utils import run_bass_kernel_spmd as _run

    nc = _bacc.Bacc("TRN2", target_bir_lowering=False, num_devices=1)
    arrays, args = {}, []
    for name in _INS:
        a = _np.ascontiguousarray(inputs[name])
        arrays[f"in_{name}"] = a
        args.append(nc.dram_tensor(f"in_{name}", a.shape, _mybir.dt.from_np(a.dtype), kind="ExternalInput").ap())
    shape = arrays["in_x"].shape
    args.append(nc.dram_tensor("out_0", shape, _mybir.dt.float32, kind="ExternalOutput").ap())
    graph_stack(nc, *args)
    r = _run(nc, [arrays], core_ids=[0])
    return r.results[0]["out_0"]
```

```python
import concourse.bass as bass
from concourse import mybir
from contextlib import ExitStack


def graph_stack(nc, x_in, adj, alpha, w0, b0, w_in, w_out, w1, b1, w2, b2, w3, a_self, a_neigh, b3, out):
    f32, f16 = mybir.dt.float32, mybir.dt.float16
    ALU = mybir.AluOpType
    ACT = mybir.ActivationFunctionType
    AX = mybir.AxisListType
    ds = bass.ds

    P = 128
    N, D = x_in.shape
    NB = N // P
    HEADS = w3.shape[0]
    C = w3.shape[2]
    EPS = 1e-5
    NEG_MASK = 1e10
    LEAK = 0.2
    LOWEST = -3.0e38

    NS = NB // 2
    NCH = 4
    MC = NB // NCH
    J = NB // 2
    SPC = J // NCH
    CW = MC * P
    W = 2 * P
    K3 = N // 512
    U3 = 2 * K3
    J_TAKE, J_DEG, J_E1, J_RELU, J_NORM = 1, 2, 3, 4, 8
    J_X0 = J // 2
    J_P3 = J_NORM + 2
    assert U3 == J
    SPLIT = {2 * n + 1: divmod(n, 2) for n in range(2 * NCH)}

    def unit_at(s, j):
        return (s - 1 if j >= J_P3 else s - 2), (j - J_P3) % J

    NQ = NB // 4
    NH = NQ // 2
    Q = 4
    QW = Q * P
    LOW, HIGH = list(range(NCH // 2)), list(range(NCH // 2, NCH))
    PARTS = [(0, 0, LOW + HIGH, []), (0, 1, HIGH + LOW, LOW),
             (1, 1, HIGH, []), (1, 0, LOW + HIGH, HIGH),
             (2, 0, LOW, []), (2, 1, LOW + HIGH, [])]

    def uses(c, part):
        return NH * sum(c in chunks for _, _, chunks, _ in PARTS[:part])

    KV = 4
    VW = N // KV
    G4 = NB // 4
    PIECES = HEADS * KV
    FUSED = [0, PIECES - 1]
    LEAKED = [i for i in range(PIECES) if i not in FUSED]
    ACT_PLAN = "L1 T01 L2 O0 L3 T10 T11 L4 T20 T21 L5 T30 T31 L6 T40 T41 X0 X1"
    DVE_PLAN = "F0 S0 V00 S1 S2 O0 S3 S4 F7 S5 S6 V50 V51 S7 V60 M0 V61 V70 V71 N0"
    FIRST_BY_DVE = [LEAKED[1], LEAKED[3]]
    BY_ACT = [(int(t[1]), int(t[2])) for t in ACT_PLAN.split() if t[0] == "T"]
    BY_DVE = [(int(t[1]), int(t[2])) for t in DVE_PLAN.split() if t[0] == "V"]
    assert sorted(BY_ACT + BY_DVE) == [(g, h) for g in range(G4) for h in range(HEADS)]

    at_dram = nc.dram_tensor("at_parts", [P + NS * NCH * P, MC * 2 * W], f16, kind="Internal").ap()
    at_dram = at_dram[P:, :].rearrange("(s c p) x -> s c p x", c=NCH, p=P)

    ctx = ExitStack()
    with ctx:
        arena = ctx.enter_context(nc.sbuf_tensor("arena", [P, 12 * NB * P], f32))

        def view(at, size, dt=f32):
            v = arena[:, int(at * NB * P):int((at + size) * NB * P)]
            return v if dt is f32 else v.bitcast(dt)

        def sb(name, shape, dt=f32):
            return ctx.enter_context(nc.sbuf_tensor(name, shape, dt))

        x_nat = view(0, 1).rearrange("p (b d) -> p b d", d=D)
        at_x1 = view(1, 1)
        y_nat = view(1, 1).rearrange("p (b d) -> p b d", d=D)
        op_even = view(2, 1, f16).rearrange("p (b l d) -> p b l d", l=2, d=D)
        op_odd = view(3, 1, f16).rearrange("p (b l d) -> p b l d", l=2, d=D)
        a_in = view(4, 2).rearrange("p (c r m) -> p c r m", c=NCH, r=2)
        split = [view(8, 2, f16).rearrange("p (r l m) -> p r l m", r=2, l=2),
                 view(6, 2, f16).rearrange("p (r l m) -> p r l m", r=2, l=2)]
        at_out = view(10, 2, f16).rearrange("p (c m l w) -> p c m l w", c=NCH, m=MC, l=2)
        at_in = view(8, 4, f16).rearrange("p (c s m l w) -> p c s m l w", c=NCH, s=2, m=MC, l=2)
        t_bcast = view(4, 2).rearrange("p (h m) -> p h m", h=HEADS)
        feats = view(6, 1).rearrange("p (b d) -> p b d", d=D)
        mask = [view(2 + k, 1) for k in range(2)]
        biased = [view((7, 7.25, 1.5, 1.75)[k], VW / N) for k in range(4)]
        t_whole = [view(7.5 + k * VW / N, VW / N) for k in range(len(FUSED))]
        prob = [[view(8 + 2 * k + h, 1) for h in range(HEADS)] for k in range(2)]
        pt = [[view(1 + (2 * k + h) * 4 / NB, 4 / NB) for h in range(HEADS)] for k in range(2)]
        stage_c = view(7 + 10 / NB, 4 / NB)
        partial = view(4.5, 0.5)
        w0_sb = view(3, 1 / NB)
        win_sb, wout_sb, w1_sb, w2_sb, w3_sb, b1_b, b2_b = (
            view(7 + k / NB, 1 / NB) for k in range(7))
        neigh_b = view(7 + 8 / NB, 2 / NB).rearrange("p (h m) -> p h m", h=HEADS)

        ident = sb("ident", [P, P])
        w0t = sb("w0t", [P, P])
        b0_b = sb("b0_b", [P, P])
        b3_b = b0_b
        self_col = sb("self_col", [P, HEADS])
        a_cols = sb("a_cols", [P, 2])
        al = sb("al", [P, 2])
        half_neg = sb("half_neg", [P, NB])
        row_part = sb("row_part", [P, NB, NCH])
        col_part = sb("col_part", [P, NB, NS])
        rows = sb("rows", [P, NB])
        cols = sb("cols", [P, NB])
        inv_rows = sb("inv_rows", [P, NB])
        inv_cols = sb("inv_cols", [P, NB])
        d_nat = sb("d_nat", [P, NB])
        guard = sb("guard", [P, NB])
        inv0 = sb("inv0", [P, 4, 2])
        stage_a = sb("stage_a", [P, QW])
        stage_b = sb("stage_b", [P, QW])
        u_t = sb("u_t", [P, Q, D])
        v_t = sb("v_t", [P, Q, D])
        x1_st = [sb(f"x1_st{k}", [P, 2, 2, D], f16) for k in range(2)]
        stats = sb("stats", [P, Q, 6])
        mv = sb("mv", [P, Q, 2])
        var_e = sb("var_e", [P, Q])
        rstd = sb("rstd", [P, Q])
        s_nat = sb("s_nat", [P, NB, HEADS])
        row_max = sb("row_max", [P, HEADS, KV])
        neg_max = sb("neg_max", [P, 2, HEADS])
        row_sum = sb("row_sum", [P, NB, HEADS])
        inv_sum = sb("inv_sum", [P, HEADS])
        moment = sb("moment", [P, 1])

        ps = ctx.enter_context(nc.psum_tensor("ps", [P, 8 * 512], f32))
        bank = [ps[:, k * 512:(k + 1) * 512] for k in range(8)]
        tp_f = bank[0:4]
        ax_f = bank[4]
        atx_f = bank[5:7]
        ep_f = bank[7]
        part_acc = bank[6]
        ep = bank[2:6]
        leak_ps = [ps[:, k * 1024:k * 1024 + VW] for k in range(2)]
        tp_j = bank[4:6]
        av_j = bank[6]
        o_j = bank[7]

        def sem(name):
            return ctx.enter_context(nc.semaphore(name))

        s_const = sem("const_loaded")
        s_ident = sem("ident_ready")
        s_pool = sem("pool_setup")
        s_w0t = sem("w0t_transposed")
        s_set = sem("dve_setup")
        x0_hi, s_x0 = sem("x0_hi"), sem("x0_split")
        x_loaded = [sem(f"x_loaded{c}") for c in range(NCH)]
        a_loaded = [sem(f"a_loaded{c}") for c in range(NCH)]
        at_stored = [sem(f"at_stored{c}") for c in range(NCH)]
        t_done, hi_done, lo_done = sem("a_transposed"), sem("at_hi"), sem("at_lo")
        sp_hi, sp_lo = sem("split_hi"), sem("split_lo")
        ax_done, qt_done = sem("ax_done"), sem("ax_taken")
        x0s_done, x0t_done, x0e_done = sem("x0_scaled"), sem("x0_transposed"), sem("x0t_taken")
        e1_done, var_f, rstd_f, x1_done, op1_done = (
            sem(n) for n in ("e1_done", "var_f", "rstd_f", "x1_done", "op1_done"))
        atx_done, atx_added = sem("atx_done"), sem("atx_added")
        ADDED_0 = K3
        link_f = sem("link_f")
        s_fin = sem("degrees_link")
        s_dpow = sem("degrees_pow")
        at_loaded = [sem(f"at_loaded{c}") for c in range(NCH)]
        at_used = [sem(f"at_used{c}") for c in range(NCH)]
        acc_taken = sem("acc_taken")
        acc_done, part_kept = sem("acc_done"), sem("part_kept")
        ea_done = sem("ea_done")
        side_taken = sem("side_taken")
        var_q, rstd_q, mid_done = sem("var_q"), sem("rstd_q"), sem("mid_done")
        eb_done, eb_taken = sem("eb_done"), sem("eb_taken")
        ec_done, ops_done = sem("ec_done"), sem("ops_done")
        link_q = sem("link_q")
        feat_t_taken, feat_done, ed_done, t_taken = (
            sem(n) for n in ("feat_t_taken", "feat_done", "ed_done", "t_taken"))
        s_late, s_neigh = sem("late_loaded"), sem("neigh_ready")
        m_loaded = [sem(f"m_loaded{k}") for k in range(2)]
        masked, bias_pool, bias_dve, fused = sem("masked"), sem("biased_by_pool"), sem("biased_by_dve"), sem("fused")
        t_whole_ready = sem("t_whole_ready")
        leaked, scored = sem("leaked"), sem("scored")
        max_done, exp_done = sem("max_done"), sem("exp_done")
        tp_done = [sem(f"tp_done{h}") for h in range(HEADS)]
        tp_act, tp_dve = sem("tp_by_act"), sem("tp_by_dve")
        av_done, o_taken, o_done = sem("av_done"), sem("o_taken"), sem("o_done")
        var_j, rstd_j, y_done, y_out = sem("var_j"), sem("rstd_j"), sem("y_done"), [sem(f"y_out{k}") for k in range(2)]
        link_j = sem("link_j")

        EARLY, LATE = 3 + 2 * HEADS, 6 + 2 * HEADS

        class Count:

            def __init__(self, engine, name, first):
                self.engine, self.reg = engine, engine.alloc_register(name)
                engine.reg_mov(self.reg, first)

            def wait(self, sem, step):
                self.engine.wait_ge(sem, self.reg)
                self.engine.reg_add(self.reg, self.reg, step)

        def acc(i):
            return bank[i % 2] if isinstance(i, int) else ps[:, ds((i % 2) * 512, 512)]

        def shares(part):
            return NH * sum(bool(ahead) for _, _, _, ahead in PARTS[:part])

        def adds_share(part):
            return part > 0 and shares(part) > shares(part - 1)

        def wait_acc(engine, part, i):
            _, _, chunks, ahead = PARTS[part]
            if ahead:
                engine.wait_ge(acc_done, shares(part) + i + 1)
            else:
                engine.wait_ge(at_used[chunks[-1]], uses(chunks[-1], part) + i + 1)

        def scored_at(b, n):
            return PIECES * (b - (n < 0)) + LEAKED[n % len(LEAKED)] + 1

        def biased_at(par, n):
            return biased[(par * len(LEAKED) + n) % 4]

        block = ctx.enter_context(nc.Block())

        @block.sync
        def _(sp):
            def load_a(s, c):
                sp.dma_start(a_in[:, c], adj[ds(s * W, W), c * CW:(c + 1) * CW]
                             .rearrange("(r p) m -> p r m", p=P)).then_inc(a_loaded[c], 16)

            early = [(w0_sb, w0), (al[:, 0:1], alpha.partition_broadcast(P)), (b0_b[:], b0.partition_broadcast(P))]
            for h in range(HEADS):
                early.append((a_cols[h * C:(h + 1) * C, 0:1], a_self[h].unsqueeze(1)))
                early.append((a_cols[h * C:(h + 1) * C, 1:2], a_neigh[h].unsqueeze(1)))
            assert len(early) == EARLY
            for c in range(NCH):
                load_a(0, c)
                sp.dma_start(x_nat[:, c * MC:(c + 1) * MC, :],
                             x_in[c * CW:(c + 1) * CW, :].rearrange("(b p) d -> p b d", p=P)).then_inc(x_loaded[c], 16)
                if c == 0:
                    for to, of in early:
                        sp.dma_start(to, of).then_inc(s_const, 16)

            def super_f(s, last=False):
                for c in range(NCH):
                    sp.wait_ge(lo_done, s * J + (c + 1) * SPC)
                    sp.dma_start(at_dram[ds(s, 1), c].rearrange("o p x -> (o p) x"),
                                 at_out[:, c].rearrange("p m l w -> p (m l w)")).then_inc(at_stored[c], 16)
                    if not last:
                        sp.wait_ge(sp_lo, s * NCH + c + 1)
                        load_a(s + 1, c)

            super_f(0)
            with sp.Fori(1, NS - 1) as s:
                super_f(s)
            super_f(NS - 1, last=True)

            def load_at(q, c):
                sp.dma_start(at_in[:, c].rearrange("p s m l w -> p s (m l w)"),
                             at_dram[ds(2 * q, 2), c].rearrange("s p x -> p s x")).then_inc(at_loaded[c], 16)

            sp.wait_ge(atx_done, U3 * (NS - 1))
            for c in range(2):
                sp.wait_ge(at_stored[c], 16 * NS)
                load_at(0, c)
            sp.wait_ge(ax_done, J * NS)
            for c in range(NCH):
                sp.wait_ge(at_stored[c], 16 * NS)
            for c in range(2, NCH):
                load_at(0, c)
            sp.wait_ge(atx_done, U3 * NS)
            late = [(win_sb, w_in), (wout_sb, w_out), (w1_sb, w1), (w2_sb, w2),
                    (b1_b, b1.partition_broadcast(P)), (b2_b, b2.partition_broadcast(P))]
            for h in range(HEADS):
                late.append((w3_sb[:, h * C:(h + 1) * C], w3[h]))
                late.append((b3_b[:, h * C:(h + 1) * C], b3[h].partition_broadcast(P)))
            assert len(late) == LATE
            for to, of in late:
                sp.dma_start(to, of).then_inc(s_late, 16)

            def load_mask(b, k):
                sp.dma_start(mask[k], adj[ds(b * P, P), :]).then_inc(m_loaded[k], 16)

            for part, (ph, half, chunks, _) in enumerate(PARTS):
                if part == 5:
                    sp.wait_ge(at_used[NCH - 1], uses(NCH - 1, 4))
                    load_mask(0, 0)
                def load_quad(i):
                    for c in chunks:
                        sp.wait_ge(at_used[c], uses(c, part) + i)
                        load_at(half * NH + i, c)

                if part == 0:
                    for i in range(1, NH):
                        load_quad(i)
                else:
                    with sp.Fori(0, NH) as i:
                        load_quad(i)

            def rows_out(b, k):
                sp.wait_ge(y_done, b + 1)
                sp.dma_start(out[ds(b * P, P), :], v_t[:, k, :]).then_inc(y_out[k], 16)

            sp.wait_ge(at_used[NCH - 1], uses(NCH - 1, 6))
            load_mask(1, 1)
            for b in range(2):
                sp.wait_ge(scored, (b + 1) * HEADS * KV)
                load_mask(b + 2, b)
            with sp.Fori(1, NB // 2 - 1) as it:
                for k in range(2):
                    b = 2 * it + k
                    sp.wait_ge(scored, (b + 1) * HEADS * KV)
                    load_mask(b + 2, k)
                    rows_out(b - 2, k)
            for b in range(NB - 4, NB):
                rows_out(b, b % 2)
            for k in range(2):
                sp.wait_ge(y_out[k], 16 * (NB // 2))

        @block.gpsimd
        def _(pool):
            nc.gpsimd.memset(ident[:], 0.0).then_inc(s_pool, 1)
            nc.gpsimd.memset(half_neg[:], -0.5).then_inc(s_pool, 1)
            pool.wait_ge(s_pool, 2)
            nc.gpsimd.affine_select(out=ident[:], in_=ident[:], compare_op=ALU.not_equal, fill=1.0, base=0,
                                    pattern=[[-1, P]], channel_multiplier=1).then_inc(s_ident, 1)

            def rsqrt_f(s):
                pool.wait_ge(var_f, s + 1)
                nc.gpsimd.tensor_tensor(rstd[:, 0:2], var_e[:, 0:2], half_neg[:, 0:2], ALU.pow).then_inc(rstd_f, 1)

            def super_f(s, par, first=False):
                for c in range(NCH):
                    pool.wait_ge(sp_hi, (s * NCH + c + 1) * 2)
                    cc = slice(c * CW, (c + 1) * CW)
                    nc.gpsimd.tensor_tensor(split[par][:, :, 1, cc], a_in[:, c], split[par][:, :, 0, cc],
                                            ALU.subtract).then_inc(sp_lo, 1)
                    if c == 0 and not first:
                        rsqrt_f(s - 1)

            super_f(0, 0, first=True)
            super_f(1, 1)
            with pool.Fori(1, NS // 2) as it:
                for k in range(2):
                    super_f(2 * it + k, k)
            rsqrt_f(NS - 1)
            pool.wait_ge(s_fin, 5)
            nc.gpsimd.tensor_tensor(d_nat[:], cols[:], half_neg[:], ALU.pow).then_inc(s_dpow, 1)

            for ph, lots in ((0, NQ), (2, NQ)):
                with pool.Fori(0, lots) as q:
                    pool.wait_ge(var_q, (NQ if ph else 0) + q + 1)
                    nc.gpsimd.tensor_tensor(rstd[:], var_e[:], half_neg[:, 0:Q], ALU.pow).then_inc(rstd_q, 1)

            def mask_piece(par, k):
                piece = mask[par][:, k * VW:(k + 1) * VW]
                nc.gpsimd.tensor_scalar(piece, piece, -1.0, NEG_MASK, ALU.add, ALU.mult).then_inc(masked, 1)

            def bias_piece(b, par, i):
                h, k = divmod(i, KV)
                vs = slice(k * VW, (k + 1) * VW)
                piece = mask[par][:, vs]
                if i in FUSED:
                    return
                n = LEAKED.index(i)
                pool.wait_ge(masked, b * KV + (k + 1 if h == 0 else KV))
                if not (isinstance(b, int) and b == 0 and n < 4):
                    pool.wait_ge(scored, scored_at(b, n - 4))
                nc.gpsimd.tensor_tensor(biased_at(par, n), piece, t_bcast[:, h, vs], ALU.add).then_inc(bias_pool, 1)

            def block_j(b, par, rsqrt_of=None):
                loads[par].wait(m_loaded[par], 16)
                for i in range(PIECES):
                    if i < KV:
                        mask_piece(par, i)
                    bias_piece(b, par, i)
                    if i == 5 and rsqrt_of is not None:
                        rsqrt_j(rsqrt_of)

            def rsqrt_j(b):
                pool.wait_ge(var_j, b + 1)
                nc.gpsimd.tensor_tensor(rstd[:, 0:1], var_e[:, 0:1], half_neg[:, 0:1], ALU.pow).then_inc(rstd_j, 1)

            loads = [Count(nc.gpsimd, f"mask_loads{k}", 16) for k in range(2)]
            loads[0].wait(m_loaded[0], 16)
            for k in range(KV):
                mask_piece(0, k)
            pool.wait_ge(t_taken, NQ)
            for i in range(PIECES):
                if i not in FIRST_BY_DVE:
                    bias_piece(0, 0, i)
            block_j(1, 1)
            with pool.Fori(1, NB // 2) as it:
                for k in range(2):
                    block_j(2 * it + k, k, rsqrt_of=2 * it + k - 2)
            rsqrt_j(NB - 2)
            rsqrt_j(NB - 1)

        @block.scalar
        def _(act):
            act.wait_ge(s_set, 1)

            def hi_parts(s, j):
                c, jj = divmod(j, SPC)
                act.wait_ge(t_done, s * J + j + 1)
                if jj == 0 and not (isinstance(s, int) and s == 0):
                    act.wait_ge(at_stored[c], 16 * s)
                    act.wait_ge(ax_done, (s - 1) * J + (c + 1) * SPC)
                for k in range(2):
                    op = nc.scalar.activation(at_out[:, c, 2 * jj + k, 0, :], tp_f[j % 4][:, k * W:(k + 1) * W],
                                              ACT.Copy, accum_out=col_part[:, 2 * j + k, ds(s, 1)])
                op.then_inc(hi_done, 1)

            def split_hi(s, par, c, r):
                act.wait_ge(a_loaded[c], 16 * (s + 1))
                nc.scalar.activation(split[par][:, r, 0, c * CW:(c + 1) * CW], a_in[:, c, r, :], ACT.Copy,
                                     accum_out=row_part[:, ds(2 * s + r, 1), c]).then_inc(sp_hi, 1)

            def super_f(s, par, first=False):
                for j in range(J):
                    hi_parts(s, j)
                    if j in SPLIT:
                        c, r = SPLIT[j]
                        if r == 0 and not (isinstance(s, int) and s < 2):
                            act.wait_ge(atx_done, U3 * (s - 2) + (c + 1) * U3 // NCH)
                        split_hi(s, par, c, r)
                    if j == J_P3 and not first:
                        keep_x1(s - 1, 1 - par)
                    if j == J_X0:
                        if not first:
                            act.wait_ge(qt_done, s)
                        nc.scalar.activation(u_x0, x_nat[:, ds(2 * s, 2), :], ACT.Copy,
                                             scale=al[:, 1:2]).then_inc(x0s_done, 1)
                    if j == J_X0 + 1:
                        act.wait_ge(x0t_done, s + 1)
                        nc.scalar.activation(stage_b[:, 0:W], ep_f[:, 0:W], ACT.Copy).then_inc(x0e_done, 1)

            def keep_x1(s, par):
                act.wait_ge(x1_done, s + 1)
                nc.scalar.activation(op_odd[:, ds(2 * s, 2)], x1_st[par][:], ACT.Copy).then_inc(op1_done, 1)

            u_x0 = v_t[:, 2:4, :]
            super_f(0, 0, first=True)
            super_f(1, 1)
            with act.Fori(1, NS // 2) as it:
                for k in range(2):
                    super_f(2 * it + k, k)
            keep_x1(NS - 1, 1)

            def take_acc(part, i):
                wait_acc(act, part, i)
                nc.scalar.activation(stage_a[:], acc(i), ACT.Copy).then_inc(acc_taken, 1)

            def take_eb(t):
                act.wait_ge(eb_done, t + 1)
                nc.scalar.activation(stage_b[:], ep[1][:], ACT.Copy).then_inc(eb_taken, 1)

            act.wait_ge(atx_added, ADDED_0 + NS * K3)
            for part, (ph, half, _, ahead) in enumerate(PARTS):
                with act.Fori(0, NH) as i:
                    t = part * NH + i
                    q = half * NH + i
                    if not adds_share(part):
                        take_acc(part, i)
                    if ph == 0:
                        nc.scalar.activation(stage_c, at_x1[:, ds(q * QW, QW)], ACT.Copy).then_inc(side_taken, 1)
                    if ahead:
                        act.wait_ge(at_used[ahead[-1]], uses(ahead[-1], part) + i + 1)
                        nc.scalar.activation(partial[:, ds(i * QW, QW)], part_acc[:], ACT.Copy).then_inc(part_kept, 1)
                    take_eb(t)
                    if ph == 2:
                        n = t - 2 * NQ
                        act.wait_ge(ec_done, t + 1)
                        nc.scalar.activation(stage_c, ep[2][:], ACT.Copy).then_inc(feat_t_taken, 1)
                        act.wait_ge(ed_done, n + 1)
                        for h in range(HEADS):
                            nc.scalar.activation(t_bcast[:, h, ds(q * QW, QW)], ep[h][:], ACT.Copy, scale=LEAK)
                        nc.scalar.activation(s_nat[:, ds(q * Q, Q), :],
                                             ep[3][:, 0:Q * HEADS].rearrange("p (r h) -> p r h", h=HEADS),
                                             ACT.Copy, scale=1.0 - LEAK).then_inc(t_taken, 1)

            def leak(b, i):
                h, k = divmod(i, KV)
                n = LEAKED.index(i)
                if not (isinstance(b, int) and b == 0 and n < 2):
                    to = (0, n + 1) if n + 1 < len(LEAKED) else (1, 0)
                    pieces_scored.wait(scored, scored_at(to[0], to[1] - 2) - scored_at(0, n - 2))
                nc.scalar.activation(leak_ps[n % 2], t_bcast[:, h, k * VW:(k + 1) * VW], ACT.Relu,
                                     bias=s_nat[:, ds(b, 1), h], scale=(1.0 - LEAK) / LEAK).then_inc(leaked, 1)

            def expo(b, par, h):
                act.wait_ge(max_done, b * HEADS + h + 1)
                nc.scalar.activation(prob[par][h], prob[par][h], ACT.Exp, bias=neg_max[:, par, h:h + 1],
                                     accum_out=row_sum[:, ds(b, 1), h]).then_inc(exp_done, 1)

            def take_tp(b, g, h):
                act.wait_ge(tp_done[h], b * G4 + g + 1)
                if not (isinstance(b, int) and b == 0 and g < 2):
                    act.wait_ge(av_done, b * G4 + g - 1)
                nc.scalar.activation(pt[g % 2][h], tp_j[h], ACT.Copy).then_inc(tp_act, 1)

            def take_out(b):
                act.wait_ge(av_done, (b + 1) * G4)
                if not (isinstance(b, int) and b == 0):
                    act.wait_ge(o_done, b)
                nc.scalar.activation(stage_a[:, 0:P], av_j[:, 0:P], ACT.Copy).then_inc(o_taken, 1)

            def block_j(b, par, first=False, last=False):
                for step in ACT_PLAN.split():
                    what, i = step[0], int(step[1])
                    if what == "L" and not last:
                        leak(b + 1, i)
                    if what == "X" and not last:
                        expo(b + 1, 1 - par, i)
                    if what == "T":
                        take_tp(b, i, int(step[2]))
                    if what == "O" and not first:
                        take_out(b - 1)

            pieces_scored = Count(nc.scalar, "pieces_scored", scored_at(0, 0))
            act.wait_ge(t_taken, NQ)
            for i in LEAKED:
                leak(0, i)
            for h in range(HEADS):
                expo(0, 0, h)
            block_j(0, 0, first=True)
            block_j(1, 1)
            with act.Fori(1, NB // 2 - 1) as it:
                for k in range(2):
                    block_j(2 * it + k, k)
            block_j(NB - 2, 0)
            block_j(NB - 1, 1, last=True)
            take_out(NB - 1)

        @block.vector
        def _(dve):
            def split_x0(c):
                cm = slice(c * MC, (c + 1) * MC)
                dve.wait_ge(x_loaded[c], 16)
                nc.vector.tensor_copy(op_even[:, cm, 0, :], x_nat[:, cm, :]).then_inc(x0_hi, 1)
                dve.wait_ge(x0_hi, c + 1)
                nc.vector.tensor_tensor(op_even[:, cm, 1, :], x_nat[:, cm, :], op_even[:, cm, 0, :],
                                        ALU.subtract).then_inc(s_x0, 1)

            nc.vector.memset(self_col[:], 0.0).then_inc(atx_added, ADDED_0)
            split_x0(0)
            dve.wait_ge(s_const, 16 * EARLY)
            nc.vector.tensor_scalar(al[:, 1:2], al[:, 0:1], -1.0, 1.0, ALU.mult, ALU.add).then_inc(s_set, 1)
            dve.wait_ge(atx_added, ADDED_0)
            for h in range(HEADS):
                hc = slice(h * C, (h + 1) * C)
                nc.vector.tensor_copy(self_col[hc, h:h + 1], a_cols[hc, 0:1])
            dve.wait_ge(s_w0t, 1)
            nc.vector.tensor_copy(w0t[:], ep_f[:, 0:P]).then_inc(s_set, 1)

            def lo_parts(s, j):
                c, jj = divmod(j, SPC)
                dve.wait_ge(hi_done, s * J + j + 1)
                nc.vector.tensor_tensor(at_out[:, c, 2 * jj:2 * jj + 2, 1, :],
                                        tp_f[j % 4][:].rearrange("p (m w) -> p m w", m=2),
                                        at_out[:, c, 2 * jj:2 * jj + 2, 0, :], ALU.subtract).then_inc(lo_done, 1)

            def chain(base, counter):
                at = [base]

                def link(op):
                    at[0] = at[0] + 1
                    op.then_inc(counter, 1)
                    dve.wait_ge(counter, at[0])
                return link

            LINKS = 14

            def take_ax(s):
                dve.wait_ge(ax_done, (s + 1) * J)
                dve.wait_ge(x0e_done, s + 1)
                nc.vector.scalar_tensor_tensor(out=stage_a[:, 0:W], in0=ax_f[:, 0:W], scalar=al[:, 0:1],
                                               in1=stage_b[:, 0:W], op0=ALU.mult, op1=ALU.add).then_inc(qt_done, 1)

            def degree(s, part):
                link = chain(s * LINKS + 4 * part, link_f)
                if part == 0:
                    dve.wait_ge(sp_hi, (s + 1) * NCH * 2)
                    link(nc.vector.tensor_reduce(rows[:, ds(2 * s, 2)], row_part[:, ds(2 * s, 2), :], AX.X, ALU.add))
                    link(nc.vector.tensor_scalar(inv0[:, 0, :], rows[:, ds(2 * s, 2)], al[:, 0:1], al[:, 1:2],
                                                 ALU.mult, ALU.add))
                    link(nc.vector.tensor_scalar(inv0[:, 1, :], inv0[:, 0, :], 0.0, None, ALU.is_equal))
                    link(nc.vector.tensor_tensor(inv0[:, 2, :], inv0[:, 0, :], inv0[:, 1, :], ALU.add))
                else:
                    link(nc.vector.reciprocal(inv0[:, 3, :], inv0[:, 2, :]))
                    link(nc.vector.tensor_tensor(inv0[:, 0, :], inv0[:, 3, :], inv0[:, 1, :], ALU.mult))
                    link(nc.vector.tensor_tensor(inv0[:, 3, :], inv0[:, 3, :], inv0[:, 0, :], ALU.subtract))

            def stats_f(s, part):
                link = chain(s * LINKS + (7, 8, 10)[part], link_f)
                if part == 0:
                    dve.wait_ge(e1_done, s + 1)
                    for r in range(2):
                        op = nc.vector.scalar_tensor_tensor(out=u_t[:, r, :], in0=ep_f[:, r * P:(r + 1) * P],
                                                            scalar=inv0[:, 3, r:r + 1], in1=b0_b[:],
                                                            op0=ALU.mult, op1=ALU.add)
                    link(op)
                if part == 1:
                    link(nc.vector.scalar_tensor_tensor(out=u_t[:, 0:2, :], in0=u_t[:, 0:2, :], scalar=0.0,
                                                        in1=x_nat[:, ds(2 * s, 2), :], op0=ALU.max, op1=ALU.add))
                    for r in range(2):
                        op = nc.vector.bn_stats(stats[:, r, :], u_t[:, r, :])
                    link(op)
                    nc.vector.memset(moment[:], 0.0)
                if part == 2:
                    for r in range(2):
                        op = nc.vector.bn_aggr(mv[:, r, :], stats[:, r, :])
                    link(op)
                    nc.vector.tensor_scalar(var_e[:, 0:2], mv[:, 0:2, 1], EPS, None, ALU.add).then_inc(var_f, 1)

            def norm_f(s, par, part):
                link = chain(s * LINKS + 11 + 2 * part, link_f)
                if part == 0:
                    dve.wait_ge(rstd_f, s + 1)
                    for r in range(2):
                        op = nc.vector.tensor_scalar(v_t[:, r, :], u_t[:, r, :], mv[:, r, 0:1], rstd[:, r:r + 1],
                                                     ALU.subtract, ALU.mult)
                    link(op)
                    dve.wait_ge(x0s_done, s + 1)
                    link(nc.vector.tensor_scalar(x_nat[:, ds(2 * s, 2), :], v_t[:, 0:2, :], 1.0, None, ALU.mult))
                else:
                    if not (isinstance(s, int) and s < 2):
                        dve.wait_ge(atx_done, U3 * (s - 1))
                        dve.wait_ge(op1_done, s - 1)
                    link(nc.vector.tensor_copy(x1_st[par][:, :, 0, :], v_t[:, 0:2, :]))
                    nc.vector.tensor_tensor(x1_st[par][:, :, 1, :], v_t[:, 0:2, :], x1_st[par][:, :, 0, :],
                                            ALU.subtract).then_inc(x1_done, 1)

            def add_atx(s, k):
                n = s * K3 + k
                dve.wait_ge(atx_done, s * U3 + 2 * k + 2)
                if not (isinstance(s, int) and s == 0):
                    dve.wait_ge(atx_added, ADDED_0 + n - K3 + 1)
                piece = at_x1[:, k * 512:(k + 1) * 512]
                nc.vector.tensor_tensor(piece, atx_f[k % 2][:], piece, ALU.add).then_inc(atx_added, 1)

            EPILOGUE = {J_TAKE: take_ax, J_DEG: lambda s: degree(s, 0), J_DEG + 1: lambda s: degree(s, 1)}
            EPILOGUE |= {J_RELU + k: (lambda s, k=k: stats_f(s, k)) for k in range(3)}

            def super_f(s, par):
                for j in range(J):
                    lo_parts(s, j)
                    if isinstance(s, int) and s == 0:
                        if j % SPC == 1 and j < J - SPC:
                            split_x0(j // SPC + 1)
                        if j == J - 2:
                            nc.vector.memset(at_x1, 0.0)
                    else:
                        if j in EPILOGUE:
                            EPILOGUE[j](s - 1)
                        if j in (J_NORM, J_NORM + 1):
                            norm_f(s - 1, 1 - par, j - J_NORM)
                    of, u = unit_at(s, j)
                    if u % 2 and not (isinstance(of, int) and of < 0):
                        add_atx(of, u // 2)

            super_f(0, 0)
            super_f(1, 1)
            with dve.Fori(1, NS // 2) as it:
                for k in range(2):
                    super_f(2 * it + k, k)
            for j in (J_DEG, J_DEG + 1, J_TAKE, J_RELU, J_RELU + 1, J_RELU + 2):
                EPILOGUE[j](NS - 1)
            norm_f(NS - 1, 1, 0)
            norm_f(NS - 1, 1, 1)
            for j in range(J_P3):
                of, u = unit_at(NS, j)
                if u % 2:
                    add_atx(of, u // 2)
            for k in range(K3):
                add_atx(NS - 1, k)

            n_fin = [0]

            def link(op):
                n_fin[0] += 1
                op.then_inc(s_fin, 1)
                dve.wait_ge(s_fin, n_fin[0])

            def where_positive(to, of):
                link(nc.vector.tensor_scalar(guard[:], of, 0.0, None, ALU.is_gt))
                link(nc.vector.tensor_tensor(to, of, guard[:], ALU.mult))
                link(nc.vector.tensor_scalar(inv_cols[:], guard[:], -1.0, 1.0, ALU.mult, ALU.add))
                link(nc.vector.tensor_tensor(to, to, inv_cols[:], ALU.add))

            link(nc.vector.tensor_scalar(inv_rows[:], rows[:], 1.0, None, ALU.add))
            where_positive(cols[:], inv_rows[:])
            assert n_fin[0] == 5
            dve.wait_ge(s_dpow, 1)
            link(nc.vector.tensor_tensor(d_nat[:], d_nat[:], guard[:], ALU.mult))
            dve.wait_ge(hi_done, NS * J)
            link(nc.vector.tensor_reduce(cols[:], col_part[:], AX.X, ALU.add))
            where_positive(inv_rows[:], rows[:])
            link(nc.vector.reciprocal(inv_rows[:], inv_rows[:]))
            where_positive(rows[:], cols[:])
            link(nc.vector.reciprocal(inv_cols[:], rows[:]))
            dve.wait_ge(s_late, 16 * LATE)
            link(nc.vector.memset(neigh_b, 0.0))
            for h in range(HEADS):
                hc = slice(h * C, (h + 1) * C)
                op = nc.vector.tensor_copy(neigh_b[hc, h, :], a_cols[hc, 1:2].to_broadcast([C, P]))
            op.then_inc(s_neigh, 1)

            LG, LH, LI = 8, 5, 6

            def layernorm_in(link):
                for r in range(Q):
                    op = nc.vector.bn_stats(stats[:, r, :], u_t[:, r, :])
                link(op)
                nc.vector.memset(moment[:], 0.0)
                for r in range(Q):
                    op = nc.vector.bn_aggr(mv[:, r, :], stats[:, r, :])
                link(op)
                nc.vector.tensor_scalar(var_e[:], mv[:, :, 1], EPS, None, ALU.add).then_inc(var_q, 1)

            def layernorm_out(link, q, n, t):
                dve.wait_ge(rstd_q, n)
                for r in range(Q):
                    op = nc.vector.tensor_scalar(v_t[:, r, :], u_t[:, r, :], mv[:, r, 0:1], rstd[:, r:r + 1],
                                                 ALU.subtract, ALU.mult)
                op.then_inc(mid_done, 1)
                dve.wait_ge(mid_done, t + 1)
                link(nc.vector.tensor_scalar(x_nat[:, ds(Q * q, Q), :], v_t[:], 1.0, None, ALU.mult))

            def operands(link, q, t, to):
                dve.wait_ge(ec_done, t + 1)
                for r in range(Q):
                    op = nc.vector.tensor_scalar(u_t[:, r, :], ep[2][:, r * P:(r + 1) * P],
                                                 d_nat[:, ds(Q * q + r, 1)], None, ALU.mult)
                link(op)
                link(nc.vector.tensor_scalar(y_nat[:, ds(Q * q, Q), :], u_t[:], 1.0, None, ALU.mult))
                link(nc.vector.tensor_scalar(to[:, ds(Q * q, Q), 0, :], u_t[:], 1.0, None, ALU.mult))
                nc.vector.tensor_tensor(to[:, ds(Q * q, Q), 1, :], u_t[:], to[:, ds(Q * q, Q), 0, :],
                                        ALU.subtract).then_inc(ops_done, 1)
                dve.wait_ge(ops_done, t + 1)

            def layer_1(t, q):
                link = chain(t * LG, link_q)
                dve.wait_ge(ea_done, t + 1)
                for r in range(Q):
                    op = nc.vector.scalar_tensor_tensor(out=u_t[:, r, :], in0=ep[0][:, r * P:(r + 1) * P],
                                                        scalar=inv_rows[:, ds(Q * q + r, 1)],
                                                        in1=x_nat[:, ds(Q * q + r, 1), :].rearrange("p o d -> p (o d)"),
                                                        op0=ALU.mult, op1=ALU.add)
                link(op)
                for r in range(Q):
                    op = nc.vector.scalar_tensor_tensor(out=u_t[:, r, :], in0=ep[3][:, r * P:(r + 1) * P],
                                                        scalar=inv_cols[:, ds(Q * q + r, 1)], in1=u_t[:, r, :],
                                                        op0=ALU.mult, op1=ALU.add)
                link(op)
                layernorm_in(link)
                layernorm_out(link, q, t + 1, t)
                return lambda: operands(link, q, t, op_even)

            def layer_2a(t, q):
                link = chain(NQ * LG + (t - NQ) * LH, link_q)
                dve.wait_ge(ea_done, t + 1)
                yq = y_nat[:, ds(Q * q, Q), :]
                link(nc.vector.tensor_tensor(u_t[:], ep[0][:].rearrange("p (r d) -> p r d", r=Q), yq, ALU.add))
                for r in range(Q):
                    op = nc.vector.scalar_tensor_tensor(out=v_t[:, r, :], in0=u_t[:, r, :],
                                                        scalar=d_nat[:, ds(Q * q + r, 1)], in1=b1_b[:],
                                                        op0=ALU.mult, op1=ALU.add)
                link(op)
                nc.vector.tensor_scalar(v_t[:], v_t[:], 0.0, None, ALU.max).then_inc(mid_done, 1)
                return lambda: operands(link, q, t, op_odd)

            def layer_2b(t, q):
                link = chain(NQ * (LG + LH) + (t - 2 * NQ) * LI, link_q)
                dve.wait_ge(ea_done, t + 1)
                yq = y_nat[:, ds(Q * q, Q), :]
                link(nc.vector.tensor_tensor(u_t[:], ep[0][:].rearrange("p (r d) -> p r d", r=Q), yq, ALU.add))
                for r in range(Q):
                    op = nc.vector.scalar_tensor_tensor(out=u_t[:, r, :], in0=u_t[:, r, :],
                                                        scalar=d_nat[:, ds(Q * q + r, 1)], in1=b2_b[:],
                                                        op0=ALU.mult, op1=ALU.add)
                link(op)
                link(nc.vector.tensor_tensor(u_t[:], u_t[:], x_nat[:, ds(Q * q, Q), :], ALU.add))
                layernorm_in(link)
                layernorm_out(link, q, t - NQ + 1, t)

                def features():
                    dve.wait_ge(feat_done, t - 2 * NQ + 1)
                    nc.vector.tensor_scalar(feats[:, ds(Q * q, Q), :], ep[3][:].rearrange("p (r d) -> p r d", r=Q), 1.0,
                                            None, ALU.mult).then_inc(ops_done, 1)
                return features

            def add_share(part, i):
                wait_acc(dve, part, i)
                dve.wait_ge(part_kept, shares(part) - NH + i + 1)
                nc.vector.tensor_tensor(stage_a[:], acc(i), partial[:, ds(i * QW, QW)], ALU.add).then_inc(acc_taken, 1)

            for part, (ph, half, _, _) in enumerate(PARTS):
                rows_of = (layer_1, layer_2a, layer_2b)[ph]
                if adds_share(part):
                    add_share(part, 0)
                with dve.Fori(0, NH - 1) as i:
                    finish = rows_of(part * NH + i, half * NH + i)
                    if adds_share(part):
                        add_share(part, i + 1)
                    finish()
                rows_of(part * NH + NH - 1, half * NH + NH - 1)()

            def free_probs(b, h):
                if not (isinstance(b, int) and b < 2):
                    dve.wait_ge(tp_done[h], (b - 1) * G4)

            def fuse(b, par, i):
                h, k = divmod(i, KV)
                vs = slice(k * VW, (k + 1) * VW)
                free_probs(b, h)
                nc.vector.scalar_tensor_tensor(out=prob[par][h][:, vs], in0=t_whole[FUSED.index(i)],
                                               scalar=s_nat[:, ds(b, 1), h], in1=t_bcast[:, h, vs],
                                               op0=ALU.add, op1=ALU.max).then_inc(fused, 1)

            def score(b, par, i):
                h, k = divmod(i, KV)
                vs = slice(k * VW, (k + 1) * VW)
                if i in FUSED:
                    dve.wait_ge(masked, b * KV + (k + 1 if h == 0 else KV))
                    pieces_fused.wait(fused, 1)
                    leaky, bias = prob[par][h][:, vs], mask[par][:, vs]
                else:
                    n = LEAKED.index(i)
                    free_probs(b, h)
                    if isinstance(b, int) and b == 0 and i in FIRST_BY_DVE:
                        dve.wait_ge(masked, KV)
                        nc.vector.tensor_tensor(biased_at(par, n), mask[par][:, vs], t_bcast[:, h, vs],
                                                ALU.add).then_inc(bias_dve, 1)
                        dve.wait_ge(bias_dve, FIRST_BY_DVE.index(i) + 1)
                    else:
                        before = len(FIRST_BY_DVE) if not (isinstance(b, int) and b == 0) else \
                            sum(f < i for f in FIRST_BY_DVE)
                        dve.wait_ge(bias_pool, b * len(LEAKED) + n + 1 - before)
                    pieces_leaked.wait(leaked, 1)
                    leaky, bias = leak_ps[n % 2], biased_at(par, n)
                nc.vector.tensor_tensor_reduce(out=prob[par][h][:, vs], in0=leaky, in1=bias,
                                               scale=1.0, scalar=LOWEST, op0=ALU.add, op1=ALU.max,
                                               accum_out=row_max[:, h, k:k + 1]).then_inc(scored, 1)

            def maximum(b, par, h):
                dve.wait_ge(scored, b * HEADS * KV + (h + 1) * KV)
                if not (isinstance(b, int) and b < 2):
                    dve.wait_ge(exp_done, (b - 1) * HEADS)
                nc.vector.tensor_reduce(neg_max[:, par, h:h + 1], row_max[:, h, :], AX.X, ALU.max,
                                        negate=True).then_inc(max_done, 1)

            def take_tp(b, g, h):
                dve.wait_ge(tp_done[h], b * G4 + g + 1)
                if not (isinstance(b, int) and b == 0 and g < 2):
                    dve.wait_ge(av_done, b * G4 + g - 1)
                nc.vector.tensor_copy(pt[g % 2][h], tp_j[h]).then_inc(tp_dve, 1)

            LJ = 5

            def stats_j(b, par):
                link = chain(b * LJ, link_j)
                dve.wait_ge(o_done, b + 1)
                link(nc.vector.reciprocal(inv_sum[:], row_sum[:, ds(b, 1), :].rearrange("p o h -> p (o h)")))
                for h in range(HEADS):
                    hc = slice(h * C, (h + 1) * C)
                    op = nc.vector.scalar_tensor_tensor(out=u_t[:, 0, hc], in0=o_j[:, hc], scalar=inv_sum[:, h:h + 1],
                                                        in1=b3_b[:, hc], op0=ALU.mult, op1=ALU.add)
                link(op)
                link(nc.vector.scalar_tensor_tensor(out=u_t[:, 0, :], in0=u_t[:, 0, :], scalar=0.0,
                                                    in1=x_nat[:, ds(b, 1), :].rearrange("p o d -> p (o d)"),
                                                    op0=ALU.max, op1=ALU.add))
                link(nc.vector.bn_stats(stats[:, 0, :], u_t[:, 0, :]))
                nc.vector.memset(moment[:], 0.0)
                link(nc.vector.bn_aggr(mv[:, 0, :], stats[:, 0, :]))
                nc.vector.tensor_scalar(var_e[:, 0:1], mv[:, 0, 1:2], EPS, None, ALU.add).then_inc(var_j, 1)

            def norm_j(b, n, par):
                dve.wait_ge(rstd_j, b + 1)
                if not (isinstance(n, int) and n == 0):
                    dve.wait_ge(y_out[par], 16 * n)
                nc.vector.tensor_scalar(v_t[:, par, :], u_t[:, 0, :], mv[:, 0, 0:1], rstd[:, 0:1],
                                        ALU.subtract, ALU.mult).then_inc(y_done, 1)

            def block_j(b, n, par, first=False, last=False):
                for step in DVE_PLAN.split():
                    what, i = step[0], int(step[1])
                    if what == "F" and not last:
                        fuse(b + 1, 1 - par, i)
                    if what == "S" and not last:
                        score(b + 1, 1 - par, i)
                        if i == KV:
                            maximum(b + 1, 1 - par, 0)
                    if what == "M" and not last:
                        maximum(b + 1, 1 - par, 1)
                    if what == "V":
                        take_tp(b, i, int(step[2]))
                    if what == "O" and not first:
                        stats_j(b - 1, 1 - par)
                    if what == "N" and not first:
                        norm_j(b - 1, n - (1 - par), 1 - par)

            pieces_leaked = Count(nc.vector, "pieces_leaked", 1)
            pieces_fused = Count(nc.vector, "pieces_fused", 1)
            dve.wait_ge(t_taken, NQ)
            for k, i in enumerate(FUSED):
                h, kk = divmod(i, KV)
                op = nc.vector.tensor_scalar(t_whole[k], t_bcast[:, h, kk * VW:(kk + 1) * VW], 1.0 / LEAK, None,
                                             ALU.mult)
            op.then_inc(t_whole_ready, 1)
            dve.wait_ge(t_whole_ready, 1)
            for i in range(HEADS * KV):
                if i in FUSED:
                    fuse(0, 0, i)
                score(0, 0, i)
                if i % KV == KV - 1:
                    maximum(0, 0, i // KV)
            block_j(0, 0, 0, first=True)
            block_j(1, 0, 1)
            with dve.Fori(1, NB // 2 - 1) as it:
                for k in range(2):
                    block_j(2 * it + k, it, k)
            block_j(NB - 2, NB // 2 - 1, 0)
            block_j(NB - 1, NB // 2 - 1, 1, last=True)
            stats_j(NB - 1, 1)
            norm_j(NB - 1, NB // 2 - 1, 1)

        @block.tensor
        def _(pe):
            pe.wait_ge(s_ident, 1)

            def transposes(s, j):
                c, jj = divmod(j, SPC)
                if jj == 0:
                    pe.wait_ge(a_loaded[c], 16 * (s + 1))
                if not (isinstance(s, int) and s == 0 and j < 4):
                    pe.wait_ge(lo_done, s * J + j - 3)
                for k in range(2):
                    for r in range(2):
                        m = (2 * jj + k) * P
                        op = nc.tensor.transpose(tp_f[j % 4][:, k * W + r * P:k * W + (r + 1) * P],
                                                 a_in[:, c, r, m:m + P], ident[:])
                op.then_inc(t_done, 1)

            def ax_step(s, j):
                c, jj = divmod(j, SPC)
                pe.wait_ge(lo_done, s * J + j + 1)
                if isinstance(s, int) and s == 0 and j % SPC == 0:
                    pe.wait_ge(s_x0, c + 1)
                if j == 0 and not (isinstance(s, int) and s == 0):
                    pe.wait_ge(qt_done, s)
                for k in range(2):
                    m = 2 * j + k
                    hi, lo = (at_out[:, c, 2 * jj + k, z, :] for z in range(2))
                    nc.tensor.matmul(ax_f[:, 0:W], op_even[:, m, 0, :], hi, start=(m == 0), stop=False)
                    nc.tensor.matmul(ax_f[:, 0:W], op_even[:, m, 0, :], lo, start=False, stop=False)
                    op = nc.tensor.matmul(ax_f[:, 0:W], op_even[:, m, 1, :], hi, start=False, stop=(m == NB - 1))
                op.then_inc(ax_done, 1)

            def layer0(s):
                pe.wait_ge(qt_done, s + 1)
                for r in range(2):
                    op = nc.tensor.matmul(ep_f[:, r * P:(r + 1) * P], stage_a[:, r * P:(r + 1) * P], w0t[:],
                                          start=True, stop=True)
                op.then_inc(e1_done, 1)

            def x0_transposed(s):
                if isinstance(s, int) and s == 0:
                    pe.wait_ge(s_set, 2)
                pe.wait_ge(x0s_done, s + 1)
                if not (isinstance(s, int) and s == 0):
                    pe.wait_ge(var_f, s)
                for r in range(2):
                    op = nc.tensor.transpose(ep_f[:, r * P:(r + 1) * P], v_t[:, 2 + r, :], ident[:])
                op.then_inc(x0t_done, 1)

            def atx_unit(s, par, u):
                k, r = divmod(u, 2)
                if u == 0:
                    pe.wait_ge(x1_done, s + 1)
                if r == 0:
                    pe.wait_ge(sp_lo, s * NCH + ((k + 1) * 512 - 1) // CW + 1)
                    if not (isinstance(s, int) and s == 0 and k < 2):
                        pe.wait_ge(atx_added, ADDED_0 + s * K3 + k - 1)
                hi, lo = (split[par][:, r, z, k * 512:(k + 1) * 512] for z in range(2))
                nc.tensor.matmul(atx_f[k % 2], x1_st[par][:, r, 0, :], hi, start=(r == 0), stop=False)
                nc.tensor.matmul(atx_f[k % 2], x1_st[par][:, r, 0, :], lo, start=False, stop=False)
                nc.tensor.matmul(atx_f[k % 2], x1_st[par][:, r, 1, :], hi, start=False, stop=(r == 1)).then_inc(atx_done, 1)

            def super_f(s, par):
                for j in range(J):
                    transposes(s, j)
                    if isinstance(s, int) and s == 0 and j == 0:
                        pe.wait_ge(s_const, 16 * EARLY)
                        nc.tensor.transpose(ep_f[:, 0:P], w0_sb, ident[:]).then_inc(s_w0t, 1)
                    of, u = unit_at(s, j)
                    if not (isinstance(of, int) and of < 0):
                        atx_unit(of, 1 - par if j >= J_P3 else par, u)
                    if j >= 2:
                        ax_step(s, j - 2)
                    elif not (isinstance(s, int) and s == 0):
                        ax_step(s - 1, J - 2 + j)
                    if j == J_E1 and not (isinstance(s, int) and s == 0):
                        layer0(s - 1)
                    if j == J_X0 + 1:
                        x0_transposed(s)

            super_f(0, 0)
            super_f(1, 1)
            with pe.Fori(1, NS // 2) as it:
                for k in range(2):
                    super_f(2 * it + k, k)
            ax_step(NS - 1, J - 2)
            ax_step(NS - 1, J - 1)
            for j in range(J_P3):
                if j == J_TAKE + 1:
                    layer0(NS - 1)
                of, u = unit_at(NS, j)
                atx_unit(of, 0, u)
            for u in range(U3):
                atx_unit(NS - 1, 1, u)

            def made(ph, j):
                part = [(p[0], p[1]) for p in PARTS].index((ph - 1, j // NH))
                return part * NH + j % NH + 1

            def products(to, ph, c, z, first, last, new):
                y = (op_odd, op_even, op_odd)[ph]
                if new and ph == 0:
                    pe.wait_ge(op1_done, NS)
                if new and ph:
                    pe.wait_ge(ops_done, made(ph, 2 * c + z))
                to = to.rearrange("p (s w) -> p s w", s=2)
                for k in range(MC // 2):
                    m = z * MC // 2 + k
                    b = c * MC + m
                    hi, lo = (at_in[:, c, :, m, l, :] for l in range(2))
                    nc.tensor.matmul(to, y[:, b, 0, :], hi, start=first and k == 0, stop=False)
                    nc.tensor.matmul(to, y[:, b, 0, :], lo, start=False, stop=False)
                    op = nc.tensor.matmul(to, y[:, b, 1, :], hi, start=False, stop=last and k == MC // 2 - 1)
                return op

            def four(to, of, weights):
                for r in range(Q):
                    op = nc.tensor.matmul(to[:, r * P:(r + 1) * P], of[:, r * P:(r + 1) * P], weights,
                                          start=True, stop=True)
                return op

            def four_transposes(to, of):
                for r in range(Q):
                    op = nc.tensor.transpose(to[:, r * P:(r + 1) * P], of(r), ident[:])
                return op

            def epilogue_a(ph, t):
                pe.wait_ge(acc_taken, t + 1)
                if ph == 0:
                    pe.wait_ge(side_taken, t + 1)
                    four(ep[3], stage_c, wout_sb)
                    four(ep[0], stage_a, win_sb).then_inc(ea_done, 1)
                else:
                    if ph == 2 and not (isinstance(t, int) and t == 2 * NQ):
                        pe.wait_ge(t_taken, t - 2 * NQ)
                    four_transposes(ep[0], lambda r: stage_a[:, r * P:(r + 1) * P]).then_inc(ea_done, 1)

            def epilogue_b(ph, t):
                pe.wait_ge(mid_done, t + 1)
                four_transposes(ep[1], lambda r: v_t[:, r, :]).then_inc(eb_done, 1)

            def epilogue_c(ph, t):
                pe.wait_ge(eb_taken, t + 1)
                if not (isinstance(t, int) and t == 0):
                    pe.wait_ge(ops_done, t)
                if ph < 2:
                    four(ep[2], stage_b, (w1_sb, w2_sb)[ph]).then_inc(ec_done, 1)
                    return
                nc.tensor.matmul(ep[2], w3_sb, stage_b[:], start=True, stop=True).then_inc(ec_done, 1)
                four(ep[3], stage_b, w3_sb).then_inc(feat_done, 1)
                pe.wait_ge(feat_t_taken, t - 2 * NQ + 1)
                for h in range(HEADS):
                    nc.tensor.matmul(ep[h], neigh_b[:, h, :], stage_c, start=True, stop=True)
                pe.wait_ge(ops_done, t + 1)
                for r in range(Q):
                    op = nc.tensor.matmul(ep[3][:, r * HEADS:(r + 1) * HEADS], stage_c[:, r * P:(r + 1) * P],
                                          self_col[:], start=True, stop=True)
                op.then_inc(ed_done, 1)

            def quad(part, i, before=None):
                assert MC == 2 * Q
                ph, _, chunks, ahead = PARTS[part]
                t = part * NH + i
                start = isinstance(i, int) and i == 0
                halves = [(c, z) for c in chunks for z in range(2)]
                end = len(halves) - 1
                at_a, at_b, at_c = 0, 3, end
                if len(chunks) < NCH and start:
                    at_b = at_c = 2
                if not (isinstance(t, int) and t < 2):
                    pe.wait_ge(acc_taken, t - 1)
                for n, (c, z) in enumerate(halves):
                    if z == 0:
                        pe.wait_ge(at_loaded[c], 16 * (uses(c, part) + i + 1))
                    op = products(acc(i), ph, c, z, n == 0, n == end, start)
                    if z == 1 and c not in ahead:
                        op.then_inc(at_used[c], 1)
                    if n == end and ahead:
                        op.then_inc(acc_done, 1)
                    for at, step in ((at_a, epilogue_a), (at_b, epilogue_b), (at_c, epilogue_c)):
                        if n == at and before:
                            step(*before)
                    if z == 1 and c in ahead:
                        if c == ahead[0] and (shares(part) or not start):
                            pe.wait_ge(part_kept, shares(part) + i)
                        for zz in range(2):
                            op = products(part_acc, ph + 1, c, zz, c == ahead[0] and zz == 0,
                                          c == ahead[-1] and zz == 1, start)
                        op.then_inc(at_used[c], 1)

            for part, (ph, _, _, _) in enumerate(PARTS):
                if part == 0:
                    quad(0, 0)
                    pe.wait_ge(s_late, 16 * LATE)
                    pe.wait_ge(atx_added, ADDED_0 + NS * K3)
                else:
                    quad(part, 0, (PARTS[part - 1][0], part * NH - 1))
                if part == 4:
                    pe.wait_ge(s_neigh, 1)
                with pe.Fori(1, NH) as i:
                    quad(part, i, (ph, part * NH + i - 1))
            for step in (epilogue_a, epilogue_b, epilogue_c):
                step(2, 3 * NQ - 1)

            def taken(b, g, h):
                for by, counter in ((BY_ACT, tp_act), (BY_DVE, tp_dve)):
                    if (g, h) in by:
                        pe.wait_ge(counter, b * len(by) + by.index((g, h)) + 1)

            def tp_group(b, par, g):
                for h in range(HEADS):
                    if g == 0:
                        pe.wait_ge(exp_done, b * HEADS + h + 1)
                        if not (isinstance(b, int) and b == 0):
                            taken(b - 1, G4 - 1, h)
                    else:
                        taken(b, g - 1, h)
                    for k in range(4):
                        m = (4 * g + k) * P
                        op = nc.tensor.transpose(tp_j[h][:, k * P:(k + 1) * P], prob[par][h][:, m:m + P], ident[:])
                    op.then_inc(tp_done[h], 1)

            def av_group(b, g):
                for h in range(HEADS):
                    taken(b, g, h)
                if g == 0 and not (isinstance(b, int) and b == 0):
                    pe.wait_ge(o_taken, b)
                for k in range(4):
                    m = 4 * g + k
                    for h in range(HEADS):
                        hc = slice(h * C, (h + 1) * C)
                        op = nc.tensor.matmul(av_j[hc, 0:P], feats[:, m, hc], pt[g % 2][h][:, k * P:(k + 1) * P],
                                              start=(m == 0), stop=(m == NB - 1))
                op.then_inc(av_done, 1)

            def out_rows(b):
                pe.wait_ge(o_taken, b + 1)
                if not (isinstance(b, int) and b == 0):
                    pe.wait_ge(var_j, b)
                nc.tensor.transpose(o_j[:, 0:P], stage_a[:, 0:P], ident[:]).then_inc(o_done, 1)

            def block_j(b, par, first=False):
                for g in range(G4):
                    tp_group(b, par, g)
                    if g == 1 and not first:
                        out_rows(b - 1)
                    if g >= 1:
                        av_group(b, g - 1)
                av_group(b, G4 - 1)

            pe.wait_ge(ops_done, 3 * NQ)
            block_j(0, 0, first=True)
            block_j(1, 1)
            with pe.Fori(1, NB // 2) as it:
                for k in range(2):
                    block_j(2 * it + k, k)
            out_rows(NB - 1)


_INS = ["x", "adj", "L0_gnn_alpha", "L0_gnn_W", "L0_gnn_b", "L1_gnn_W_in", "L1_gnn_W_out", "L2_gnn_W1", "L2_gnn_b1",
        "L2_gnn_W2", "L2_gnn_b2", "L3_gnn_W", "L3_gnn_a_self", "L3_gnn_a_neigh", "L3_gnn_b"]


def kernel(**inputs):
    import numpy as _np
    import concourse.bacc as _bacc
    from concourse import mybir as _mybir
    from concourse.bass_utils import run_bass_kernel_spmd as _run

    nc = _bacc.Bacc("TRN2", target_bir_lowering=False, num_devices=1)
    arrays, args = {}, []
    for name in _INS:
        a = _np.ascontiguousarray(inputs[name])
        arrays[f"in_{name}"] = a
        args.append(nc.dram_tensor(f"in_{name}", a.shape, _mybir.dt.from_np(a.dtype), kind="ExternalInput").ap())
    shape = arrays["in_x"].shape
    args.append(nc.dram_tensor("out_0", shape, _mybir.dt.float32, kind="ExternalOutput").ap())
    graph_stack(nc, *args)
    r = _run(nc, [arrays], core_ids=[0])
    return r.results[0]["out_0"]
```
